# Optimizing a Trainium2 kernel written in Bass

```python
import numpy as np
import jax
import jax.numpy as jnp

def _softmax(x, axis=-1):
    return jax.nn.softmax(x, axis=axis)

def _gelu(x):
    return jax.nn.gelu(x, approximate=True)

def _silu(x):
    return jax.nn.silu(x)

def _sigmoid(x):
    return jax.nn.sigmoid(x)

def _layernorm(x, axis=-1, eps=1e-05):
    m = jnp.mean(x, axis=axis, keepdims=True)
    v = jnp.var(x, axis=axis, keepdims=True)
    return (x - m) / jnp.sqrt(v + eps)

def _scatter_add(tgt, idx, src, axis=0):
    return tgt.at[idx].add(src)

def _segment_sum(src, seg, n):
    return jax.ops.segment_sum(src, seg, n)
kernel_name = 'mk_decoder_postln_d1_seqx_r4_72132e'

def setup_inputs(seed: int=0):
    np.random.seed(seed)
    _w = jnp.asarray

    def _rec_inputs():
        import jax
        import jax.numpy as jnp
        _rk = jax.random.key(seed)
        x = -0.0005207 + 1.001 * jax.random.normal(jax.random.fold_in(_rk, 1), (16, 128, 256), jnp.float32)
        _lenS = 128 - jax.random.randint(jax.random.fold_in(_rk, 7), (16,), 0, max(1, 128 // 4) + 1, jnp.int32)
        _lenS2 = 128 - jax.random.randint(jax.random.fold_in(_rk, 8), (16,), 0, max(1, 128 // 4) + 1, jnp.int32)
        _ctx_512P = jax.random.normal(jax.random.fold_in(_rk, 11), (16, 16, 128), jnp.float32)
        _ctx_512c = jax.random.dirichlet(jax.random.fold_in(_rk, 511), 0.3 * jnp.ones((16,), jnp.float32), (16, 128))
        _ctx_512t = jnp.einsum('bsk,bkd->bsd', _ctx_512c, _ctx_512P)
        _ctx_512t = _ctx_512t * jax.lax.rsqrt(jnp.mean(jnp.square(_ctx_512t)) + 1e-12) * 0.953939
        ctx_512 = 0.502058 + 0.29099 * (_ctx_512t + 0.3 * jax.random.normal(jax.random.fold_in(_rk, 611), (16, 128, 128), jnp.float32))
        itok_BxS2xS_0_7 = jax.random.randint(jax.random.fold_in(_rk, 12), (16, 128, 128), 0, 8, jnp.int32)
        return (x, ctx_512, itok_BxS2xS_0_7)
    x, ctx_512, itok_BxS2xS_0_7 = _rec_inputs()

    def _L0_attn_setup():
        import math
        import jax, jax.numpy as jnp
        import numpy as np
        D_MODEL = 256
        NUM_HEADS = 16
        D_HEAD = D_MODEL // NUM_HEADS
        K_S = 32
        B, N = (2, 512)

        def _attn(x, Wq, bq, Wk, bk, Wv, bv, Wo, bo):
            b, n, _ = x.shape
            q = (x @ Wq.T + bq).reshape(b, n, NUM_HEADS, D_HEAD).transpose(0, 2, 1, 3)
            k = (x @ Wk.T + bk).reshape(b, n, NUM_HEADS, D_HEAD).transpose(0, 2, 1, 3)
            v = (x @ Wv.T + bv).reshape(b, n, NUM_HEADS, D_HEAD).transpose(0, 2, 1, 3)
            scores = jnp.einsum('bhqd,bhkd->bhqk', q, k) / math.sqrt(D_HEAD)
            causal = jnp.triu(jnp.ones((n, n), dtype=bool), k=1)
            neg_inf = jnp.array(-jnp.inf, dtype=scores.dtype)
            scores = jnp.where(causal, neg_inf, scores)
            vals, idx = jax.lax.top_k(scores, K_S)
            masked = jnp.full_like(scores, -jnp.inf)
            masked = jnp.put_along_axis(masked, idx, vals, axis=-1, inplace=False)
            attn = jax.nn.softmax(masked, axis=-1)
            out = jnp.einsum('bhqk,bhkd->bhqd', attn, v)
            out = out.transpose(0, 2, 1, 3).reshape(b, n, D_MODEL)
            y = out @ Wo.T + bo
            return (y, attn.mean(axis=1))

        def _reference_tuple_inner(x, Wq, bq, Wk, bk, Wv, bv, Wo, bo):
            return _attn(x, Wq, bq, Wk, bk, Wv, bv, Wo, bo)
        key = jax.random.key(seed)
        ks = jax.random.split(key, 9)
        s = 1.0 / math.sqrt(D_MODEL)
        return {'x': jax.random.normal(ks[0], (B, N, D_MODEL), dtype=jnp.float32), 'Wq': jax.random.normal(ks[1], (D_MODEL, D_MODEL), dtype=jnp.float32) * s, 'bq': jnp.zeros((D_MODEL,), dtype=jnp.float32), 'Wk': jax.random.normal(ks[2], (D_MODEL, D_MODEL), dtype=jnp.float32) * s, 'bk': jnp.zeros((D_MODEL,), dtype=jnp.float32), 'Wv': jax.random.normal(ks[3], (D_MODEL, D_MODEL), dtype=jnp.float32) * s, 'bv': jnp.zeros((D_MODEL,), dtype=jnp.float32), 'Wo': jax.random.normal(ks[4], (D_MODEL, D_MODEL), dtype=jnp.float32) * s, 'bo': jnp.zeros((D_MODEL,), dtype=jnp.float32)}
    _L0_attn_all = _L0_attn_setup()
    _L0_attn_in = {k: v for k, v in _L0_attn_all.items() if k in ('Wq', 'bq', 'Wk', 'bk', 'Wv', 'bv', 'Wo', 'bo')}
    del _L0_attn_all

    def _L0_xattn_setup():
        import jax, jax.numpy as jnp
        import numpy as np
        key = jax.random.key(seed)
        k1, k2, k3, k4, k5 = jax.random.split(key, 5)
        B, K, S, E, I, D = (4, 2, 128, 8, 256, 512)
        x = jax.random.normal(k1, (B, S, I), dtype=jnp.float32)
        weights = jax.random.uniform(k2, (B, K, S), dtype=jnp.float32)
        ensembles = jax.random.randint(k3, (B, K, S), 0, E, dtype=jnp.int64)
        lim1 = float(np.sqrt(6.0 / (D + I)))
        proj_in = jax.random.uniform(k4, (E, D, I), dtype=jnp.float32, minval=-lim1, maxval=lim1)
        proj_out = jax.random.uniform(k5, (E, I, D), dtype=jnp.float32, minval=-lim1, maxval=lim1)
        return {'x': x, 'weights': weights, 'ensembles': ensembles, 'proj_in': proj_in, 'proj_out': proj_out}
    _L0_xattn_all = _L0_xattn_setup()
    _L0_xattn_in = {k: v for k, v in _L0_xattn_all.items() if k in ('proj_in', 'proj_out')}
    del _L0_xattn_all

    def _L0_ffn_setup():
        import jax, jax.numpy as jnp
        import numpy as np
        IN_FEATURES = 256
        ACT_BITS = 4

        def _hadamard(size: int) -> np.ndarray:
            h = np.array([[1.0]], dtype=np.float64)
            while h.shape[0] < size:
                h = np.block([[h, h], [h, -h]])
            return (h / np.sqrt(size)).astype(np.float32)

        def _quantize_activations(x, bits=ACT_BITS):
            pos = 2 ** (bits - 1) - 1
            neg = 2 ** (bits - 1)
            scale = jnp.clip(jnp.max(jnp.abs(jax.lax.stop_gradient(x)), axis=-1, keepdims=True), 1e-05) / pos
            q = jnp.clip(jnp.round(x / scale), -neg, pos) * scale
            return x + jax.lax.stop_gradient(q - x)

        def _ternary_quantize_ste(w):
            scale = jnp.clip(jnp.mean(jnp.abs(jax.lax.stop_gradient(w)), axis=1, keepdims=True), 1e-05)
            n = w / scale
            tern = jnp.where(n > 0.5, 1.0, jnp.where(n < -0.5, -1.0, 0.0))
            q = tern * scale
            return w + jax.lax.stop_gradient(q - w)
        key = jax.random.key(seed)
        k1, k2 = jax.random.split(key)
        x = jax.random.normal(k1, (8, 2048, IN_FEATURES), dtype=jnp.float32)
        bound = 1.0 / np.sqrt(IN_FEATURES)
        weight = jax.random.uniform(k2, (256, IN_FEATURES), dtype=jnp.float32, minval=-bound, maxval=bound)
        return {'x': x, 'weight': weight}
    _L0_ffn_all = _L0_ffn_setup()
    _L0_ffn_in = {k: v for k, v in _L0_ffn_all.items() if k in ('weight',)}
    del _L0_ffn_all
    return {'x': x, 'ctx_512': ctx_512, 'itok_BxS2xS_0_7': itok_BxS2xS_0_7, 'L0_attn_Wq': _L0_attn_in['Wq'], 'L0_attn_bq': _L0_attn_in['bq'], 'L0_attn_Wk': _L0_attn_in['Wk'], 'L0_attn_bk': _L0_attn_in['bk'], 'L0_attn_Wv': _L0_attn_in['Wv'], 'L0_attn_bv': _L0_attn_in['bv'], 'L0_attn_Wo': _L0_attn_in['Wo'], 'L0_attn_bo': _L0_attn_in['bo'], 'L0_xattn_proj_in': _L0_xattn_in['proj_in'], 'L0_xattn_proj_out': _L0_xattn_in['proj_out'], 'L0_ffn_weight': _L0_ffn_in['weight']}

def reference(x, ctx_512, itok_BxS2xS_0_7, L0_attn_Wq, L0_attn_bq, L0_attn_Wk, L0_attn_bk, L0_attn_Wv, L0_attn_bv, L0_attn_Wo, L0_attn_bo, L0_xattn_proj_in, L0_xattn_proj_out, L0_ffn_weight):
    import jax
    import jax.numpy as jnp

    def _L0_attn_ref(x, Wq, bq, Wk, bk, Wv, bv, Wo, bo):
        import math
        import jax, jax.numpy as jnp
        import numpy as np
        D_MODEL = 256
        NUM_HEADS = 16
        D_HEAD = D_MODEL // NUM_HEADS
        K_S = 32
        B, N = (2, 512)

        def _attn(x, Wq, bq, Wk, bk, Wv, bv, Wo, bo):
            b, n, _ = x.shape
            q = (x @ Wq.T + bq).reshape(b, n, NUM_HEADS, D_HEAD).transpose(0, 2, 1, 3)
            k = (x @ Wk.T + bk).reshape(b, n, NUM_HEADS, D_HEAD).transpose(0, 2, 1, 3)
            v = (x @ Wv.T + bv).reshape(b, n, NUM_HEADS, D_HEAD).transpose(0, 2, 1, 3)
            scores = jnp.einsum('bhqd,bhkd->bhqk', q, k) / math.sqrt(D_HEAD)
            causal = jnp.triu(jnp.ones((n, n), dtype=bool), k=1)
            neg_inf = jnp.array(-jnp.inf, dtype=scores.dtype)
            scores = jnp.where(causal, neg_inf, scores)
            vals, idx = jax.lax.top_k(scores, K_S)
            masked = jnp.full_like(scores, -jnp.inf)
            masked = jnp.put_along_axis(masked, idx, vals, axis=-1, inplace=False)
            attn = jax.nn.softmax(masked, axis=-1)
            out = jnp.einsum('bhqk,bhkd->bhqd', attn, v)
            out = out.transpose(0, 2, 1, 3).reshape(b, n, D_MODEL)
            y = out @ Wo.T + bo
            return (y, attn.mean(axis=1))

        def _reference_tuple_inner(x, Wq, bq, Wk, bk, Wv, bv, Wo, bo):
            return _attn(x, Wq, bq, Wk, bk, Wv, bv, Wo, bo)
        return _reference_tuple_inner(x, Wq, bq, Wk, bk, Wv, bv, Wo, bo)[0]

    def _L0_xattn_ref(x, weights, ensembles, proj_in, proj_out):
        import jax, jax.numpy as jnp
        import numpy as np
        E = proj_in.shape[0]
        h = jax.nn.relu(jnp.einsum('edi,bsi->bsed', proj_in, x))
        o = jnp.einsum('eid,bsed->bsei', proj_out, h)
        onehot = jax.nn.one_hot(ensembles, E, dtype=x.dtype)
        gate = jnp.einsum('bks,bkse->bse', weights, onehot)
        return jnp.einsum('bsei,bse->bsi', o, gate)

    def _L0_ffn_ref(x, weight):
        import jax, jax.numpy as jnp
        import numpy as np
        IN_FEATURES = 256
        ACT_BITS = 4

        def _hadamard(size: int) -> np.ndarray:
            h = np.array([[1.0]], dtype=np.float64)
            while h.shape[0] < size:
                h = np.block([[h, h], [h, -h]])
            return (h / np.sqrt(size)).astype(np.float32)

        def _quantize_activations(x, bits=ACT_BITS):
            pos = 2 ** (bits - 1) - 1
            neg = 2 ** (bits - 1)
            scale = jnp.clip(jnp.max(jnp.abs(jax.lax.stop_gradient(x)), axis=-1, keepdims=True), 1e-05) / pos
            q = jnp.clip(jnp.round(x / scale), -neg, pos) * scale
            return x + jax.lax.stop_gradient(q - x)

        def _ternary_quantize_ste(w):
            scale = jnp.clip(jnp.mean(jnp.abs(jax.lax.stop_gradient(w)), axis=1, keepdims=True), 1e-05)
            n = w / scale
            tern = jnp.where(n > 0.5, 1.0, jnp.where(n < -0.5, -1.0, 0.0))
            q = tern * scale
            return w + jax.lax.stop_gradient(q - w)
        H = jnp.asarray(_hadamard(IN_FEATURES))
        xh = x @ H
        xq = _quantize_activations(xh)
        wq = _ternary_quantize_ste(weight)
        return jnp.einsum('bsi,oi->bso', xq, wq)
    x = _layernorm(x + _L0_attn_ref(x, L0_attn_Wq, L0_attn_bq, L0_attn_Wk, L0_attn_bk, L0_attn_Wv, L0_attn_bv, L0_attn_Wo, L0_attn_bo), axis=-1)
    x = _layernorm(x + _L0_xattn_ref(x, ctx_512, itok_BxS2xS_0_7, L0_xattn_proj_in, L0_xattn_proj_out), axis=-1)
    x = _layernorm(x + _L0_ffn_ref(x, L0_ffn_weight), axis=-1)
    return x

_drawn_inputs = setup_inputs


def setup_inputs(seed=0):
    import zlib

    import numpy as np

    out = dict(_drawn_inputs(seed))
    spreads = {'L0_attn_bq': (0.0, 0.1),
     'L0_attn_bk': (0.0, 0.1),
     'L0_attn_bv': (0.0, 0.1),
     'L0_attn_bo': (0.0, 0.1)}
    factors = {}
    for name, (base, spread) in spreads.items():
        noise = np.random.default_rng([zlib.crc32(name.encode()), seed]).standard_normal(out[name].shape)
        drawn = base * np.exp(spread * noise) if base else spread * noise
        out[name] = jnp.asarray(drawn.astype(out[name].dtype))
    for name, factor in factors.items():
        out[name] = (out[name] * factor).astype(out[name].dtype)
    return out
```

```python
from contextlib import ExitStack

import concourse.bass as bass
from concourse import mybir

ALU = mybir.AluOpType
ACT = mybir.ActivationFunctionType
AX_X = mybir.AxisListType.X
F32 = mybir.dt.float32
BF16 = mybir.dt.bfloat16
I32 = mybir.dt.int32

P = 128
BATCH, SEQ, D = 16, 128, 256
HEADS = 16
DH = D // HEADS
TOPK = 32
EXPERTS, HIDDEN = 8, 512
CD = D // P
CH = HIDDEN // P
UB = 2
UT = UB * SEQ
UNITS = BATCH // UB
HG = P // DH
GROUPS = HEADS // HG
TILES = UB * GROUPS
QB = P // HG
BLOCKS = SEQ // QB
FREE_BLOCKS = TOPK // QB
HALF = BLOCKS // 2
VW = DH + 1
SCALE = DH ** -0.5
EPS = 1e-5
MASKED = -1e30
TAKEN = -3e38
ROUND = 1.5 * 2.0 ** 23
QPOS, QNEG = 7, 8
RING_STEPS = 2 * EXPERTS


def block_at(j):
    return QB * j * (j + 1) // 2


def prob_at(j):
    return 64 * j if j < HALF else 64 * HALF + P * (j - HALF)


S_COLS = block_at(BLOCKS)
P_COLS = prob_at(BLOCKS)
SEL_FROM = prob_at(FREE_BLOCKS)
ROUNDS = TOPK // 8
STAGES = 2 * ROUNDS - 1
SEL_GROUP = (BLOCKS - FREE_BLOCKS) // 2
SEL_STEPS = 2 * STAGES


def expert_steps():
    steps = [("L1", 0, 0), ("L1", 0, 1)]
    for e in range(1, EXPERTS):
        steps += [("L1", e, 0), ("L2", e - 1, 0), ("L1", e, 1), ("L2", e - 1, 1)]
    return steps + [("L2", EXPERTS - 1, 0), ("L2", EXPERTS - 1, 1)]


SLOTS = 4 * EXPERTS
LAG = 14


def build_schedule():
    steps = expert_steps()
    at = [[] for _ in range(SLOTS)]

    def put(slot, engine, name, off, *args):
        at[slot].append((engine, name, off, args))

    for s in range(SLOTS):
        kind, e, i = steps[(s - LAG) % SLOTS]
        off = 1 if s >= LAG else 2
        put(s, "pe", kind, off, e, i)
        put(s, "act" if kind == "L1" else "dve", "relu" if kind == "L1" else "gated_sum", off, e, i)
    for k in range(TILES):
        b = 8 * k
        put(b, "dve", "first_max", 0, k)
        put(b, "act", "exp", 0, k)
        for r in range(STAGES):
            put(b + 1 + r, "dve", "select", 0, k, r)
        put(b + 7, "dve", "keep", 0, k)
        n, s = (k + 1, b + 1) if k < TILES - 1 else (0, b + 2)
        put(s, "pe", "scores", 0 if k < TILES - 1 else -1, n)
        put(s, "act", "copy_scores", 0 if k < TILES - 1 else -1, n)
        off, b = (0, b + 8) if k < TILES - 1 else (1, 0)
        for half in range(2):
            put(b + half, "pe", "turn_probs", off, k, half)
            put(b + half, "act", "copy_probs", off, k, half)
        put(b + 3, "pe", "attend", off, k)
        put(b + 3, "dve", "normalise", off, k)
    put(0, "sp", "load_ctx", 1)
    put(0, "sp", "load_x", 1)
    put(5, "pe", "v", 0)
    put(5, "act", "copy_v", 0)
    put(6, "sp", "load_xt", -1)
    put(4, "pool", "x_plus_bo", 1)
    put(6, "pe", "turn_o", 1)
    put(6, "act", "copy_ot", 1)
    put(7, "pe", "out_proj", 1)
    put(7, "dve", "ln1_stats", 1)
    put(7, "pool", "rstd", 1, 0)
    put(9, "dve", "ln1_apply", 1)
    put(10, "pe", "turn_x1", 1)
    put(10, "act", "copy_x1t", 1)
    put(8, "dve", "gate_masks", 1)
    put(14, "pe", "gates", 1)
    put(14, "act", "copy_gates", 1)
    put(14, "dve", "ln2_stats", 2)
    put(14, "pool", "rstd", 2, 1)
    put(15, "dve", "ln2_apply", 2)
    put(16, "pe", "turn_x2", 2)
    put(16, "act", "copy_x2t", 2)
    put(17, "pe", "hadamard", 2)
    put(17, "dve", "quantise", 2)
    put(18, "act", "to_q4", 2)
    put(20, "pe", "turn_q4", 2)
    put(20, "act", "copy_q4t", 2)
    put(21, "pe", "ffn", 2)
    put(21, "dve", "ln3_stats", 2)
    put(21, "pool", "rstd", 2, 2)
    put(23, "dve", "ln3_apply", 2)
    put(23, "sp", "store", 2)
    put(18, "pe", "q", -1)
    put(18, "act", "copy_q", -1)
    put(19, "pe", "k", -1)
    put(19, "act", "copy_k", -1)
    for k in range(TILES):
        put(22 + k, "pool", "spread_q", -1, k)
    return [x for slot in at for x in slot]


SCHEDULE = build_schedule()
FIRST_LOOP, LAST_LOOP = 2, UNITS - 2
ITERATIONS = UNITS + 2


def decoder_layer(nc, x, xt, ctx_w, itok, wqt, bq, wkt, bk, wvt, bv, wot, bo, w1t, w2t, ffnt,
                  c_ident, c_hadamard, c_causal, c_heads, out):
    with ExitStack() as stack:
        def sb(name, shape, dt=F32):
            return stack.enter_context(nc.sbuf_tensor(name, shape, dt))

        def sem(name):
            return stack.enter_context(nc.semaphore(name))

        def bank(name):
            return stack.enter_context(nc.psum_tensor(name, [P, 512], F32))

        wq_sb, wk_sb, wv_sb, wo_sb = (sb(n, [P, CD, D]) for n in ("wq_sb", "wk_sb", "wv_sb", "wo_sb"))
        bq_sb, bk_sb, bv_sb = (sb(n, [P, CD]) for n in ("bq_sb", "bk_sb", "bv_sb"))
        bo_sb = sb("bo_sb", [P, D])
        w1_sb = sb("w1_sb", [P, EXPERTS, CD, HIDDEN])
        w2_sb = sb("w2_sb", [P, EXPERTS, CH, D])
        had_sb = sb("had_sb", [P, CD, D])
        ffn_sb = sb("ffn_sb", [P, CD, D])
        tern_sb = sb("tern_sb", [P, CD, D], BF16)
        wscale = sb("wscale", [P, D])
        ident = sb("ident", [P, P])
        ident_h = sb("ident_h", [P, P], BF16)
        causal = sb("causal", [P, QB])
        causal_h = sb("causal_h", [P, QB], BF16)
        head_mask = sb("head_mask", [P, HG])
        ones = sb("ones", [P, P])
        minus_half = sb("minus_half", [P, UB])
        tmp_a = sb("tmp_a", [P, CD, D])
        tmp_b = sb("tmp_b", [P, CD, D])
        xt_sb = sb("xt_sb", [P, CD, UT])
        qt_sb = sb("qt_sb", [P, GROUPS, UT])
        kt_sb = sb("kt_sb", [P, GROUPS, UT])
        q_spread = sb("q_spread", [P, TILES, BLOCKS, HG, QB])
        v_sb = sb("v_sb", [P, UB * HEADS, VW])
        s_sb = sb("s_sb", [P, 2, S_COLS])
        top8 = sb("top8", [P, 2, BLOCKS, 8])
        next8 = sb("next8", [P, BLOCKS, 8])
        neg_max = sb("neg_max", [P, 2, BLOCKS])
        taken = sb("taken", [P, P_COLS])
        e_sb = sb("e_sb", [P, 2, P_COLS])
        p_sb = sb("p_sb", [P, 2, P_COLS])
        pt_sb = sb("pt_sb", [P, 2, HG, BLOCKS, QB])
        rsum = sb("rsum", [P, HG])
        o_sb = sb("o_sb", [P, UB, D])
        ot_sb = sb("ot_sb", [P, CD, UT])
        x_sb = sb("x_sb", [P, UB, D])
        xb_sb = sb("xb_sb", [P, UB, D])
        t1 = sb("t1", [P, UB, D])
        t3 = sb("t3", [P, UB, D])
        stats = sb("stats", [P, 3, UB, 6])
        meanvar = sb("meanvar", [P, 3, UB, 2])
        var_eps = sb("var_eps", [P, 3, UB])
        rstd = sb("rstd", [P, 3, UB])
        x1 = sb("x1", [P, UB, D])
        x1t = sb("x1t", [P, CD, UT])
        x2 = sb("x2", [P, UB, D])
        x2t = sb("x2t", [P, CD, UT])
        out_sb = sb("out_sb", [P, UB, D])
        ctx_sb = sb("ctx_sb", [P, UB, SEQ])
        itok_sb = sb("itok_sb", [P, UB, SEQ], I32)
        gmask = sb("gmask", [P, EXPERTS, UB, SEQ])
        gate = sb("gate", [P, UB, EXPERTS])
        h_sb = sb("h_sb", [P, 2, CH, UT])
        acc = sb("acc", [P, UB, D])
        amax = sb("amax", [P, UB])
        xscale = sb("xscale", [P, UB])
        xscale_inv = sb("xscale_inv", [P, UB])
        rounded = sb("rounded", [P, UB, D])
        clipped = sb("clipped", [P, UB, D])
        q4 = sb("q4", [P, UB, D], BF16)
        q4t = sb("q4t", [P, CD, UT], BF16)
        f_sb = sb("f_sb", [P, UB, D])

        ps_hi, ps_lo, ps_pt, ps_misc = bank("ps_hi"), bank("ps_lo"), bank("ps_pt"), bank("ps_misc")
        ps_z = [bank("ps_z0"), bank("ps_z1")]
        ps_o = [bank("ps_o0"), bank("ps_o1")]
        misc_h = ps_misc[:, :].bitcast(BF16)

        s_const, s_qk, s_vo, s_ffnw = sem("s_const"), sem("s_qk"), sem("s_vo"), sem("s_ffnw")
        s_w1 = [sem(f"s_w1_{e}") for e in range(EXPERTS)]
        s_w2 = [sem(f"s_w2_{e}") for e in range(EXPERTS)]
        s_xt, s_x, s_ctx, s_store = sem("xt_loaded"), sem("x_loaded"), sem("ctx_loaded"), sem("out_stored")
        zeroed, pool_const, cast_done, ffn_prep, ffn_abs, ffn_sum = (
            sem("zeroed"), sem("pool_const"), sem("cast_done"), sem("ffn_prep"), sem("ffn_abs"), sem("ffn_sum"))
        q_ready, k_ready, v_ready, s_ready, pt_ready, pv_ready = (
            sem(n) for n in ("q_ready", "k_ready", "v_ready", "s_ready", "pt_ready", "pv_ready"))
        ot_ready, y_ready, x1t_ready, g_ready, l1_done, l2_done = (
            sem(n) for n in ("ot_ready", "y_ready", "x1t_ready", "g_ready", "l1_done", "l2_done"))
        x2t_ready, xh_ready, q4t_ready, f_ready = (
            sem(n) for n in ("x2t_ready", "xh_ready", "q4t_ready", "f_ready"))
        q_copied, k_copied, v_copied, s_copied, pt_copied, ot_copied = (
            sem(n) for n in ("q_copied", "k_copied", "v_copied", "s_copied", "pt_copied", "ot_copied"))
        x1t_copied, g_copied, x2t_copied, q4t_copied, relu_done, e_ready, q4_ready = (
            sem(n) for n in ("x1t_copied", "g_copied", "x2t_copied", "q4t_copied", "relu_done", "e_ready",
                             "q4_ready"))
        max_ready, nmax_ready, sel_step, p_ready, rsum_ready, o_ready = (
            sem(n) for n in ("max_ready", "nmax_ready", "sel_step", "p_ready", "rsum_ready", "o_ready"))
        t1_ready, t3_ready, gmask_ready, acc_done, x1_ready, x2_ready, out_ready = (
            sem(n) for n in ("t1_ready", "t3_ready", "gmask_ready", "acc_done", "x1_ready", "x2_ready",
                             "out_ready"))
        stat_step = [sem(f"stat_step{i}") for i in range(3)]
        dve_held, pool_held = sem("dve_held"), sem("pool_held")
        quant_step, inv_ready, f_scaled = sem("quant_step"), sem("inv_ready"), sem("f_scaled")
        spread_ready, xb_ready = sem("spread_ready"), sem("xb_ready")
        eps_added = [sem(f"eps_added{i}") for i in range(3)]
        rstd_ready = [sem(f"rstd_ready{i}") for i in range(3)]

        MISC = {
            "q": (q_copied, 1, lambda k: 1), "k": (k_copied, 1, lambda k: 1), "v": (v_copied, 1, lambda k: 1),
            "attend": (o_ready, TILES, lambda k: k + 1), "turn_o": (ot_copied, 1, lambda k: 1),
            "out_proj": (t1_ready, 1, lambda k: 1), "turn_x1": (x1t_copied, 1, lambda k: 1),
            "gates": (g_copied, 1, lambda k: 1), "turn_x2": (x2t_copied, 1, lambda k: 1),
            "hadamard": (quant_step, 4, lambda k: 3), "turn_q4": (q4t_copied, 1, lambda k: 1),
            "ffn": (f_scaled, 1, lambda k: 1),
        }

        def walk(engine, step, eng):
            def iteration(u, inside):
                for e, name, off, args in SCHEDULE:
                    if e == engine and (inside or 0 <= u - off < UNITS):
                        step(name, u - off, off, *args)
            for u in range(-1, FIRST_LOOP):
                iteration(u, False)
            with eng.Fori(FIRST_LOOP, LAST_LOOP + 1) as u:
                iteration(u, True)
            for u in range(LAST_LOOP + 1, ITERATIONS):
                iteration(u, False)

        def wait(eng, s, value):
            if not isinstance(value, int) or value > 0:
                eng.wait_ge(s, value)

        block = stack.enter_context(nc.Block())

        @block.sync
        def _(sp):
            def rows(a):
                return a.rearrange("(c p) n -> p c n", p=P)

            def step(name, v, off, *args):
                if name == "load_xt":
                    wait(sp, v_ready, v)
                    sp.dma_start(xt_sb[:, :, :], rows(xt)[:, :, bass.ds(v * UT, UT)]).then_inc(s_xt, 16)
                elif name == "load_x":
                    wait(sp, xb_ready, v)
                    sp.dma_start(x_sb[:, :, :], x.rearrange("b s d -> s b d")[:, bass.ds(v * UB, UB), :])\
                        .then_inc(s_x, 16)
                elif name == "load_ctx":
                    wait(sp, gmask_ready, v)
                    sp.dma_start(ctx_sb[:, :, :], ctx_w.rearrange("b k s -> k b s")[:, bass.ds(v * UB, UB), :])\
                        .then_inc(s_ctx, 16)
                    sp.dma_start(itok_sb[:, :, :], itok.rearrange("b k s -> k b s")[:, bass.ds(v * UB, UB), :])\
                        .then_inc(s_ctx, 16)
                elif name == "store":
                    sp.wait_ge(out_ready, v + 1)
                    sp.dma_start(out.rearrange("b s d -> s b d")[:, bass.ds(v * UB, UB), :], out_sb[:, :, :])\
                        .then_inc(s_store, 16)

            sp.dma_start(wq_sb[:, :, :], rows(wqt)).then_inc(s_qk, 16)
            sp.dma_start(wk_sb[:, :, :], rows(wkt)).then_inc(s_qk, 16)
            for dst, src in ((bq_sb, bq), (bk_sb, bk), (bv_sb, bv)):
                sp.dma_start(dst[:, :], src[:, :]).then_inc(s_const, 16)
            sp.dma_start(bo_sb[:, :], bo.rearrange("(a n) -> a n", a=1).broadcast_to([P, D])).then_inc(s_const, 16)
            for dst, src in ((ident, c_ident), (causal, c_causal), (head_mask, c_heads)):
                sp.dma_start(dst[:, :], src[:, :]).then_inc(s_const, 16)
            sp.dma_start(wv_sb[:, :, :], rows(wvt)).then_inc(s_vo, 16)
            sp.dma_start(wo_sb[:, :, :], rows(wot)).then_inc(s_vo, 16)
            sp.dma_start(ffn_sb[:, :, :], rows(ffnt)).then_inc(s_ffnw, 16)
            sp.dma_start(had_sb[:, :, :], rows(c_hadamard)).then_inc(s_ffnw, 16)
            walk("sp", step, sp)
            sp.wait_ge(s_store, 16 * UNITS)

        CONSTS = 7 * 16

        @block.gpsimd
        def _(pool):
            nc.gpsimd.memset(minus_half[:, :], -0.5)
            nc.gpsimd.memset(ones[:, :], 1.0)
            nc.gpsimd.memset(v_sb[:, :, DH:VW], 1.0)
            nc.gpsimd.memset(pt_sb[:, :, :, :, :], 0.0).then_inc(pool_const, 1)
            pool.wait_ge(s_const, CONSTS)

            def step(name, v, off, *args):
                if name == "spread_q":
                    k, = args
                    b, g = divmod(k, GROUPS)
                    pool.wait_ge(q_copied, v + 1)
                    wait(pool, s_ready, 2 * (TILES * (v - 1) + k) + 2)
                    q_in = qt_sb[:, g, b * SEQ:(b + 1) * SEQ].rearrange("p (j a q) -> p j a q", a=1, q=QB)
                    nc.gpsimd.tensor_tensor(
                        q_spread[:, k, :, :, :], q_in.broadcast_to([P, BLOCKS, HG, QB]),
                        head_mask[:, :].rearrange("p (a h c) -> p a h c", a=1, c=1).broadcast_to([P, BLOCKS, HG, QB]),
                        ALU.mult).then_inc(spread_ready, 1)
                elif name == "x_plus_bo":
                    pool.wait_ge(s_x, 16 * (v + 1))
                    wait(pool, t1_ready, v)
                    for b in range(UB):
                        last = nc.gpsimd.tensor_tensor(xb_sb[:, b, :], x_sb[:, b, :], bo_sb[:, :], ALU.add)
                    last.then_inc(xb_ready, 1)
                elif name == "rstd":
                    i, = args
                    pool.wait_ge(stat_step[i], 2 * (v + 1))
                    pool.sem_inc(pool_held, 1)
                    nc.gpsimd.tensor_scalar(var_eps[:, i, :], meanvar[:, i, :, 1], EPS, None, ALU.add)\
                        .then_inc(eps_added[i], 1)
                    pool.wait_ge(eps_added[i], v + 1)
                    nc.gpsimd.tensor_tensor(rstd[:, i, :], var_eps[:, i, :], minus_half[:, :], ALU.pow)\
                        .then_inc(rstd_ready[i], 1)

            walk("pool", step, pool)

        @block.scalar
        def _(act):
            act.wait_ge(s_const, CONSTS)
            act.activation(ident_h[:, :], ident[:, :], ACT.Copy)
            act.activation(causal_h[:, :], causal[:, :], ACT.Copy).then_inc(cast_done, 1)
            act.wait_ge(s_ffnw, 32)
            act.activation(tmp_a[:, :, :], ffn_sb[:, :, :], ACT.Abs).then_inc(ffn_abs, 1)
            act.wait_ge(s_qk, 32)
            act.wait_ge(s_xt, 16)
            for e in range(EXPERTS):
                act.dma_start(w1_sb[:, e, :, :], w1t[e].rearrange("(c p) d -> p c d", p=P)).then_inc(s_w1[e], 16)
                act.dma_start(w2_sb[:, e, :, :], w2t[e].rearrange("(c p) i -> p c i", p=P)).then_inc(s_w2[e], 16)

            def step(name, v, off, *args):
                n = TILES * v + args[0] if name in ("exp", "copy_scores", "copy_probs") else None
                if name == "copy_q" or name == "copy_k":
                    ready, dst, bias, copied = ((q_ready, qt_sb, bq_sb, q_copied) if name == "copy_q"
                                                else (k_ready, kt_sb, bk_sb, k_copied))
                    act.wait_ge(ready, v + 1)
                    if name == "copy_q":
                        wait(act, spread_ready, TILES * v)
                    for g in range(GROUPS):
                        last = act.activation(dst[:, g, :], ps_misc[:, g * UT:(g + 1) * UT], ACT.Identity,
                                              bias=bias[:, g:g + 1])
                    last.then_inc(copied, 1)
                elif name == "copy_v":
                    act.wait_ge(v_ready, v + 1)
                    act.activation(v_sb[:, :, 0:DH], ps_misc[:, :].rearrange("p (h d) -> p h d", d=DH), ACT.Copy)\
                        .then_inc(v_copied, 1)
                elif name == "copy_scores":
                    k, = args
                    wait(act, p_ready, n - 1)
                    act.wait_ge(s_ready, 2 * n + 1)
                    act.activation(s_sb[:, k % 2, block_at(HALF):S_COLS], ps_hi[:, 0:S_COLS - block_at(HALF)],
                                   ACT.Copy).then_inc(s_copied, 1)
                    act.wait_ge(s_ready, 2 * n + 2)
                    act.activation(s_sb[:, k % 2, 0:block_at(HALF)], ps_lo[:, 0:block_at(HALF)],
                                   ACT.Copy).then_inc(s_copied, 1)
                elif name == "exp":
                    k, = args
                    act.wait_ge(nmax_ready, n + 1)
                    wait(act, p_ready, n - 1)
                    wait(act, pt_ready, 2 * n - 2)
                    for j in range(BLOCKS):
                        m = QB * (j + 1)
                        dst = p_sb if j < FREE_BLOCKS else e_sb
                        last = act.activation(dst[:, k % 2, prob_at(j):prob_at(j) + m],
                                              s_sb[:, k % 2, block_at(j):block_at(j) + m], ACT.Exp,
                                              bias=neg_max[:, k % 2, j:j + 1], scale=SCALE)
                    last.then_inc(e_ready, 1)
                elif name == "copy_probs":
                    k, half = args
                    rows = P if half else P // 2
                    act.wait_ge(pt_ready, 2 * n + half + 1)
                    wait(act, pv_ready, n - 1)
                    act.activation(
                        pt_sb[0:rows, k % 2, :, HALF * half:HALF * (half + 1), :].rearrange("p h j q -> p j h q"),
                        ps_pt[0:rows, :].rearrange("p (j h q) -> p j h q", h=HG, q=QB), ACT.Copy)\
                        .then_inc(pt_copied, 1)
                elif name == "copy_ot":
                    act.wait_ge(ot_ready, v + 1)
                    for c in range(CD):
                        last = act.activation(ot_sb[:, c, :], ps_misc[:, c * UT:(c + 1) * UT], ACT.Identity,
                                              bias=bv_sb[:, c:c + 1])
                    last.then_inc(ot_copied, 1)
                elif name in ("copy_x1t", "copy_x2t"):
                    ready, dst, copied = ((x1t_ready, x1t, x1t_copied) if name == "copy_x1t"
                                          else (x2t_ready, x2t, x2t_copied))
                    act.wait_ge(ready, v + 1)
                    act.activation(dst[:, :, :], ps_misc[:, :].rearrange("p (c t) -> p c t", c=CD), ACT.Copy)\
                        .then_inc(copied, 1)
                elif name == "copy_gates":
                    act.wait_ge(g_ready, v + 1)
                    wait(act, acc_done, RING_STEPS * v)
                    act.activation(gate[:, :, :], ps_misc[:, 0:UB * EXPERTS].rearrange("p (b e) -> p b e", b=UB),
                                   ACT.Copy).then_inc(g_copied, 1)
                elif name == "relu":
                    e, z = args
                    i = RING_STEPS * v + 2 * e + z
                    act.wait_ge(l1_done, i + 1)
                    wait(act, l2_done, RING_STEPS * v + 2 * e - 2)
                    act.activation(h_sb[:, e % 2, 2 * z:2 * z + 2, :],
                                   ps_z[z][:, :].rearrange("p (c t) -> p c t", c=2), ACT.Relu)\
                        .then_inc(relu_done, 1)
                elif name == "to_q4":
                    act.wait_ge(quant_step, 4 * (v + 1))
                    act.activation(q4[:, :, :], clipped[:, :, :], ACT.Copy, bias=-ROUND).then_inc(q4_ready, 1)
                elif name == "copy_q4t":
                    act.wait_ge(q4t_ready, v + 1)
                    act.activation(q4t[:, :, :], misc_h[:, 0:CD * UT].rearrange("p (c t) -> p c t", c=CD), ACT.Copy)\
                        .then_inc(q4t_copied, 1)

            walk("act", step, act)

        @block.tensor
        def _(pe):
            misc_before = [None]

            def take_misc(name, v, off, k=0):
                if misc_before[0] is not None:
                    s, per_unit, count, v0, off0, k0 = misc_before[0]
                    if not isinstance(v, int) and isinstance(v0, int):
                        v0 = v + (off - off0 - 1)
                    elif isinstance(v, int) and not isinstance(v0, int):
                        v0 = LAST_LOOP - off0
                    pe.wait_ge(s, v0 * per_unit + count(k0))
                misc_before[0] = (*MISC[name], v, off, k)

            def project(w, ready):
                for g in range(GROUPS):
                    for c in range(CD):
                        last = pe.matmul(ps_misc[:, g * UT:(g + 1) * UT], w[:, c, g * P:(g + 1) * P],
                                         xt_sb[:, c, :], start=c == 0, stop=c == CD - 1)
                last.then_inc(ready, 1)

            def rows_by(lhs, rhs, ready):
                for b in range(UB):
                    for c in range(CD):
                        last = pe.matmul(ps_misc[:, b * D:(b + 1) * D], lhs[:, c, b * SEQ:(b + 1) * SEQ],
                                         rhs[:, c, :], start=c == 0, stop=c == CD - 1)
                last.then_inc(ready, 1)

            def turn(src, idn, ready, dst):
                for c in range(CD):
                    for b in range(UB):
                        last = pe.transpose(dst[:, c * UT + b * SEQ:c * UT + (b + 1) * SEQ],
                                            src[:, b, c * P:(c + 1) * P], idn[:, :])
                last.then_inc(ready, 1)

            def step(name, v, off, *args):
                if name in MISC:
                    take_misc(name, v, off, *args)
                if name == "q":
                    pe.wait_ge(s_xt, 16 * (v + 1))
                    project(wq_sb, q_ready)
                elif name == "k":
                    project(wk_sb, k_ready)
                elif name == "v":
                    if off == 0 and isinstance(v, int) and v == 0:
                        pe.wait_ge(s_vo, 32)
                    rows_by(xt_sb, wv_sb, v_ready)
                elif name == "scores":
                    k, = args
                    n = TILES * v + k
                    b, g = divmod(k, GROUPS)
                    pe.wait_ge(spread_ready, n + 1)
                    pe.wait_ge(k_copied, v + 1)
                    for half, ps in ((1, ps_hi), (0, ps_lo)):
                        wait(pe, s_copied, 2 * n - half)
                        for j in range(HALF * half, HALF * (half + 1)):
                            m, at = QB * (j + 1), block_at(j) - block_at(HALF * half)
                            pe.matmul(ps[:, at:at + m],
                                      q_spread[:, k, j, :, :].rearrange("p h q -> p (h q)"),
                                      kt_sb[:, g, b * SEQ:b * SEQ + m], start=True, stop=False,
                                      skip_group_check=True)
                            last = pe.matmul(ps[:, at + m - QB:at + m], ident_h[:, :], causal_h[:, :],
                                             start=False, stop=True, skip_group_check=True)
                        last.then_inc(s_ready, 1)
                elif name == "turn_probs":
                    k, half = args
                    n = TILES * v + k
                    pe.wait_ge(p_ready, n + 1)
                    wait(pe, pt_copied, 2 * n + half)
                    for i in range(HALF):
                        at = prob_at(HALF * half + i)
                        last = pe.transpose(ps_pt[:, i * P:(i + 1) * P], p_sb[:, k % 2, at:at + P], ident[:, :])
                    last.then_inc(pt_ready, 1)
                elif name == "attend":
                    k, = args
                    n = TILES * v + k
                    b, g = divmod(k, GROUPS)
                    pe.wait_ge(pt_copied, 2 * n + 2)
                    pe.wait_ge(v_copied, v + 1)
                    for h in range(HG):
                        last = pe.matmul(ps_misc[:, h * VW:(h + 1) * VW], pt_sb[:, k % 2, h, :, :].rearrange("p j q -> p (j q)"),
                                         v_sb[:, b * HEADS + g * HG + h, :], start=True, stop=True)
                    last.then_inc(pv_ready, 1)
                elif name == "turn_o":
                    pe.wait_ge(o_ready, TILES * (v + 1))
                    turn(o_sb, ident, ot_ready, ps_misc)
                elif name == "out_proj":
                    pe.wait_ge(ot_copied, v + 1)
                    rows_by(ot_sb, wo_sb, y_ready)
                elif name == "turn_x1":
                    pe.wait_ge(x1_ready, v + 1)
                    turn(x1, ident, x1t_ready, ps_misc)
                elif name == "gates":
                    pe.wait_ge(gmask_ready, v + 1)
                    for b in range(UB):
                        for e in range(EXPERTS):
                            last = pe.matmul(ps_misc[:, b * EXPERTS + e:b * EXPERTS + e + 1], gmask[:, e, b, :],
                                             ones[:, 0:1], start=True, stop=True)
                    last.then_inc(g_ready, 1)
                elif name == "L1":
                    e, z = args
                    i = RING_STEPS * v + 2 * e + z
                    if e == 0 and z == 0:
                        pe.wait_ge(x1t_copied, v + 1)
                    if off == 2 or isinstance(v, int):
                        pe.wait_ge(s_w1[e], 16)
                    wait(pe, relu_done, i - 1)
                    for d in range(2):
                        for c in range(CD):
                            at = (2 * z + d) * P
                            last = pe.matmul(ps_z[z][:, d * UT:(d + 1) * UT], w1_sb[:, e, c, at:at + P],
                                             x1t[:, c, :], start=c == 0, stop=c == CD - 1)
                    last.then_inc(l1_done, 1)
                elif name == "L2":
                    e, b = args
                    i = RING_STEPS * v + 2 * e + b
                    pe.wait_ge(relu_done, RING_STEPS * v + 2 * e + 2)
                    if off == 2 or isinstance(v, int):
                        pe.wait_ge(s_w2[e], 16)
                    wait(pe, acc_done, i - 1)
                    for c in range(CH):
                        last = pe.matmul(ps_o[b][:, 0:D], h_sb[:, e % 2, c, b * SEQ:(b + 1) * SEQ],
                                         w2_sb[:, e, c, :], start=c == 0, stop=c == CH - 1)
                    last.then_inc(l2_done, 1)
                elif name == "turn_x2":
                    pe.wait_ge(x2_ready, v + 1)
                    turn(x2, ident, x2t_ready, ps_misc)
                elif name == "hadamard":
                    pe.wait_ge(x2t_copied, v + 1)
                    rows_by(x2t, had_sb, xh_ready)
                elif name == "turn_q4":
                    pe.wait_ge(q4_ready, v + 1)
                    turn(q4, ident_h, q4t_ready, misc_h)
                elif name == "ffn":
                    pe.wait_ge(q4t_copied, v + 1)
                    rows_by(q4t, tern_sb, f_ready)

            pe.wait_ge(pool_const, 1)
            pe.wait_ge(ffn_abs, 1)
            for c in range(CD):
                last = pe.matmul(ps_misc[:, 0:D], ones[:, :], tmp_a[:, c, :], start=c == 0, stop=c == CD - 1)
            last.then_inc(ffn_sum, 1)
            pe.wait_ge(ffn_prep, 2)
            pe.wait_ge(cast_done, 1)
            pe.wait_ge(s_qk, 32)
            walk("pe", step, pe)

        @block.vector
        def _(dve):
            V = nc.vector

            def layernorm_stats(i, src, v):
                for b in range(UB):
                    last = V.bn_stats(stats[:, i, b, :], src[:, b, :])
                last.then_inc(stat_step[i], 1)
                dve.wait_ge(stat_step[i], 2 * v + 1)
                dve.sem_inc(dve_held, 1)
                for b in range(UB):
                    last = V.bn_aggr(meanvar[:, i, b, :], stats[:, i, b, :])
                last.then_inc(stat_step[i], 1)

            def layernorm_apply(i, dst, src, v, ready):
                dve.wait_ge(rstd_ready[i], v + 1)
                for b in range(UB):
                    last = V.tensor_scalar(dst[:, b, :], src[:, b, :], meanvar[:, i, b, 0:1], rstd[:, i, b:b + 1],
                                           ALU.subtract, ALU.mult)
                last.then_inc(ready, 1)

            def step(name, v, off, *args):
                if name == "first_max":
                    k, = args
                    n = TILES * v + k
                    dve.wait_ge(s_copied, 2 * n + 2)
                    wait(dve, e_ready, n - 1)
                    dve.sem_inc(dve_held, 1)
                    for j in range(BLOCKS):
                        last = V.max(top8[:, k % 2, j, :], s_sb[:, k % 2, block_at(j):block_at(j + 1)])
                    last.then_inc(max_ready, 1)
                    dve.wait_ge(max_ready, n + 1)
                    V.tensor_scalar(neg_max[:, k % 2, :], top8[:, k % 2, :, 0], -SCALE, None, ALU.mult)\
                        .then_inc(nmax_ready, 1)
                elif name == "select":
                    k, r = args
                    n = TILES * v + k
                    if r == 0:
                        wait(dve, p_ready, n)
                    for i, j in enumerate(range(FREE_BLOCKS, BLOCKS)):
                        m = QB * (j + 1)
                        t = taken[:, prob_at(j):prob_at(j) + m]
                        if r > 0 and i % SEL_GROUP == 0:
                            dve.wait_ge(sel_step, SEL_STEPS * n + 2 * (r - 1) + i // SEL_GROUP + 1)
                        if i % SEL_GROUP == 0:
                            dve.sem_inc(dve_held, 1)
                        if r % 2 == 1:
                            last = V.max(next8[:, j, :], t)
                        elif r == 0:
                            last = V.match_replace(t, top8[:, k % 2, j, :],
                                                   s_sb[:, k % 2, block_at(j):block_at(j) + m], TAKEN)
                        else:
                            last = V.match_replace(t, next8[:, j, :], t, TAKEN)
                        if i % SEL_GROUP == SEL_GROUP - 1:
                            last.then_inc(sel_step, 1)
                elif name == "keep":
                    k, = args
                    n = TILES * v + k
                    dve.wait_ge(e_ready, n + 1)
                    dve.wait_ge(sel_step, SEL_STEPS * (n + 1))
                    wait(dve, pt_ready, 2 * n - 2)
                    V.scalar_tensor_tensor(p_sb[:, k % 2, SEL_FROM:P_COLS], taken[:, SEL_FROM:P_COLS], TAKEN,
                                           e_sb[:, k % 2, SEL_FROM:P_COLS], ALU.is_equal, ALU.mult)\
                        .then_inc(p_ready, 1)
                elif name == "normalise":
                    k, = args
                    n = TILES * v + k
                    b, g = divmod(k, GROUPS)
                    dve.wait_ge(pv_ready, n + 1)
                    wait(dve, ot_ready, v)
                    pv = ps_misc[:, 0:HG * VW].rearrange("p (h c) -> p h c", c=VW)
                    V.reciprocal(rsum[:, :], pv[:, :, DH]).then_inc(rsum_ready, 1)
                    dve.wait_ge(rsum_ready, n + 1)
                    V.tensor_tensor(o_sb[:, b, g * P:(g + 1) * P].rearrange("p (h c) -> p h c", c=DH),
                                    pv[:, :, 0:DH],
                                    rsum[:, :].rearrange("p (h a) -> p h a", a=1).broadcast_to([P, HG, DH]),
                                    ALU.mult).then_inc(o_ready, 1)
                elif name == "ln1_stats":
                    dve.wait_ge(y_ready, v + 1)
                    dve.wait_ge(xb_ready, v + 1)
                    V.tensor_tensor(t1[:, :, :], ps_misc[:, :].rearrange("p (b n) -> p b n", b=UB),
                                    xb_sb[:, :, :], ALU.add).then_inc(t1_ready, 1)
                    dve.wait_ge(t1_ready, v + 1)
                    layernorm_stats(0, t1, v)
                elif name == "ln1_apply":
                    layernorm_apply(0, x1, t1, v, x1_ready)
                elif name == "gate_masks":
                    dve.wait_ge(s_ctx, 32 * (v + 1))
                    wait(dve, g_ready, v)
                    for e in range(EXPERTS):
                        last = V.scalar_tensor_tensor(gmask[:, e, :, :], itok_sb[:, :, :], float(e),
                                                      ctx_sb[:, :, :], ALU.is_equal, ALU.mult)
                    last.then_inc(gmask_ready, 1)
                elif name == "gated_sum":
                    e, b = args
                    i = RING_STEPS * v + 2 * e + b
                    dve.wait_ge(l2_done, i + 1)
                    if e == 0:
                        dve.wait_ge(g_copied, v + 1)
                    else:
                        dve.wait_ge(acc_done, i - 1)
                    prev = x1 if e == 0 else acc
                    V.scalar_tensor_tensor(acc[:, b, :], ps_o[b][:, 0:D], gate[:, b, e:e + 1], prev[:, b, :],
                                           ALU.mult, ALU.add).then_inc(acc_done, 1)
                elif name == "ln2_stats":
                    dve.wait_ge(acc_done, RING_STEPS * (v + 1))
                    layernorm_stats(1, acc, v)
                elif name == "ln2_apply":
                    layernorm_apply(1, x2, acc, v, x2_ready)
                elif name == "quantise":
                    dve.wait_ge(xh_ready, v + 1)
                    xh = ps_misc[:, :].rearrange("p (b n) -> p b n", b=UB)
                    V.tensor_reduce(amax[:, :], xh, AX_X, ALU.max, apply_absolute_value=True)\
                        .then_inc(quant_step, 1)
                    dve.wait_ge(quant_step, 4 * v + 1)
                    V.tensor_scalar(xscale[:, :], amax[:, :], 1e-5, 1.0 / QPOS, ALU.max, ALU.mult)\
                        .then_inc(quant_step, 1)
                    dve.wait_ge(quant_step, 4 * v + 2)
                    V.reciprocal(xscale_inv[:, :], xscale[:, :]).then_inc(inv_ready, 1)
                    dve.wait_ge(inv_ready, v + 1)
                    for b in range(UB):
                        last = V.tensor_scalar(rounded[:, b, :], xh[:, b, :], xscale_inv[:, b:b + 1], ROUND,
                                               ALU.mult, ALU.add)
                    last.then_inc(quant_step, 1)
                    dve.wait_ge(quant_step, 4 * v + 3)
                    V.tensor_scalar(clipped[:, :, :], rounded[:, :, :], ROUND - QNEG, ROUND + QPOS, ALU.max,
                                    ALU.min).then_inc(quant_step, 1)
                elif name == "ln3_stats":
                    dve.wait_ge(f_ready, v + 1)
                    for b in range(UB):
                        last = V.scalar_tensor_tensor(f_sb[:, b, :], ps_misc[:, b * D:(b + 1) * D],
                                                      xscale[:, b:b + 1], wscale[:, :], ALU.mult, ALU.mult)
                    last.then_inc(f_scaled, 1)
                    dve.wait_ge(f_scaled, v + 1)
                    V.tensor_tensor(t3[:, :, :], f_sb[:, :, :], x2[:, :, :], ALU.add).then_inc(t3_ready, 1)
                    dve.wait_ge(t3_ready, v + 1)
                    layernorm_stats(2, t3, v)
                elif name == "ln3_apply":
                    wait(dve, s_store, 16 * v)
                    layernorm_apply(2, out_sb, t3, v, out_ready)

            for b in (taken, e_sb, p_sb):
                last = V.memset(b[:], 0.0)
            last.then_inc(zeroed, 1)
            dve.wait_ge(s_ffnw, 32)
            dve.wait_ge(ffn_sum, 1)
            V.tensor_scalar(wscale[:, :], ps_misc[:, 0:D], 1.0 / D, 1e-5, ALU.mult, ALU.max).then_inc(ffn_prep, 1)
            dve.wait_ge(ffn_prep, 1)
            for c in range(CD):
                V.scalar_tensor_tensor(tmp_a[:, c, :], wscale[:, :], 0.5, ffn_sb[:, c, :], ALU.mult, ALU.is_lt)
                last = V.scalar_tensor_tensor(tmp_b[:, c, :], wscale[:, :], -0.5, ffn_sb[:, c, :], ALU.mult,
                                              ALU.is_gt)
            last.then_inc(ffn_prep, 1)
            dve.wait_ge(ffn_prep, 2)
            V.tensor_tensor(tern_sb[:, :, :], tmp_a[:, :, :], tmp_b[:, :, :], ALU.subtract).then_inc(ffn_prep, 1)
            dve.wait_ge(zeroed, 1)
            walk("dve", step, dve)


_INPUTS = ["x", "xt", "ctx_w", "itok", "wqt", "bq", "wkt", "bk", "wvt", "bv", "wot", "bo", "w1t", "w2t", "ffnt",
           "c_ident", "c_hadamard", "c_causal", "c_heads"]


def kernel(x, ctx_512, itok_BxS2xS_0_7, L0_attn_Wq, L0_attn_bq, L0_attn_Wk, L0_attn_bk, L0_attn_Wv, L0_attn_bv,
           L0_attn_Wo, L0_attn_bo, L0_xattn_proj_in, L0_xattn_proj_out, L0_ffn_weight):
    import numpy as np
    import concourse.bacc as bacc
    from concourse import mybir as mb
    from concourse.bass_utils import run_bass_kernel_spmd

    had = np.array([[1.0]])
    while had.shape[0] < D:
        had = np.block([[had, had], [had, -had]])

    def by_chunk(bias):
        return np.asarray(bias).reshape(CD, P).T

    row, col = np.arange(P)[:, None], np.arange(P)[None, :]
    arrays = {
        "x": x, "xt": np.asarray(x).reshape(BATCH * SEQ, D).T, "ctx_w": ctx_512, "itok": itok_BxS2xS_0_7,
        "wqt": np.asarray(L0_attn_Wq).T, "bq": by_chunk(L0_attn_bq), "wkt": np.asarray(L0_attn_Wk).T, "bk": by_chunk(L0_attn_bk),
        "wvt": np.asarray(L0_attn_Wv).T, "bv": by_chunk(L0_attn_bv), "wot": np.asarray(L0_attn_Wo).T, "bo": L0_attn_bo,
        "w1t": np.asarray(L0_xattn_proj_in).transpose(0, 2, 1),
        "w2t": np.asarray(L0_xattn_proj_out).transpose(0, 2, 1),
        "ffnt": np.asarray(L0_ffn_weight).T,
        "c_ident": np.eye(P, dtype=np.float32),
        "c_hadamard": (had / np.sqrt(D)).astype(np.float32),
        "c_causal": np.where(col[:, :QB] > row % QB, MASKED, 0.0).astype(np.float32),
        "c_heads": (row // DH == col[:, :HG]).astype(np.float32),
    }
    arrays = {f"in_{n}": np.ascontiguousarray(arrays[n]) for n in _INPUTS}
    nc = bacc.Bacc("TRN2", target_bir_lowering=False, num_devices=1)
    args = [nc.dram_tensor(n, a.shape, mb.dt.from_np(a.dtype), kind="ExternalInput").ap() for n, a in arrays.items()]
    out = nc.dram_tensor("out", (BATCH, SEQ, D), mb.dt.float32, kind="ExternalOutput").ap()
    decoder_layer(nc, *args, out)
    r = run_bass_kernel_spmd(nc, [arrays], core_ids=[0])
    return r.results[0]["out"]
```

```python
from contextlib import ExitStack

import concourse.bass as bass
from concourse import mybir

ALU = mybir.AluOpType
ACT = mybir.ActivationFunctionType
AX_X = mybir.AxisListType.X
F32 = mybir.dt.float32
BF16 = mybir.dt.bfloat16
F16 = mybir.dt.float16
I32 = mybir.dt.int32

P = 128
BATCH, SEQ, D = 16, 128, 256
HEADS = 16
DH = D // HEADS
TOPK = 32
EXPERTS, HIDDEN = 8, 512
CD = D // P
CH = HIDDEN // P
UB = 2
UT = UB * SEQ
UNITS = BATCH // UB
HG = P // DH
GROUPS = HEADS // HG
TILES = UB * GROUPS
QB = P // HG
BLOCKS = SEQ // QB
FREE_BLOCKS = TOPK // QB
HALF = BLOCKS // 2
VW = DH + 1
SCALE = DH ** -0.5
EPS = 1e-5
MASKED = -1e30
TAKEN = -3e38
ROUND = 1.5 * 2.0 ** 23
QPOS, QNEG = 7, 8
RING_STEPS = 2 * EXPERTS
STAGED = 2
EXPONENT = 1 << 23


def block_at(j):
    return QB * j * (j + 1) // 2


def prob_at(j):
    return 64 * j if j < HALF else 64 * HALF + P * (j - HALF)


S_COLS = block_at(BLOCKS)
P_COLS = prob_at(BLOCKS)
SEL_FROM = prob_at(FREE_BLOCKS)
ROUNDS = TOPK // 8
STAGES = 2 * ROUNDS - 1
SEL_GROUP = (BLOCKS - FREE_BLOCKS) // 2
SEL_STEPS = 2 * STAGES


def expert_steps():
    steps = [("L1", 0, 0), ("L1", 0, 1)]
    for e in range(1, EXPERTS):
        steps += [("L1", e, 0), ("L2", e - 1, 0), ("L1", e, 1), ("L2", e - 1, 1)]
    return steps + [("L2", EXPERTS - 1, 0), ("L2", EXPERTS - 1, 1)]


SLOTS = 4 * EXPERTS
LAG = 11
PREP_SLOTS = 6


def build_schedule(iteration):
    steps = expert_steps()
    at = [[] for _ in range(SLOTS + 4)]

    def put(slot, engine, name, off, *args):
        at[slot].append((engine, name, off, args))

    for s in range(SLOTS):
        kind, e, i = steps[(s - LAG) % SLOTS]
        put(s, "pe", kind, 1 if s >= LAG else 2, e, i)
        if kind == "L1":
            put(s, "act", "relu", 1 if s >= LAG else 2, e, i)
            put(s, "pool", "h_low", 1 if s >= LAG else 2, e, i)
        kind, e, i = steps[(s - LAG - 2) % SLOTS]
        if kind == "L2":
            put(s, "dve", "gated_sum", 1 if s >= LAG + 2 else 2, e, i)
    for k in range(TILES):
        b = 8 * k
        put(b, "dve", "first_max", 0, k)
        put(b + 1, "act", "exp", 0, k)
        for r in range(STAGES):
            put(b + 1 + r // 2, "dve", "select", 0, k, r)
        put(b + 5, "dve", "keep", 0, k)
        n, s = (k + 1, b + 1) if k < TILES - 1 else (0, b + 2)
        put(s, "pe", "scores", 0 if k < TILES - 1 else -1, n)
        put(s + 1, "act", "copy_scores", 0 if k < TILES - 1 else -1, n)
        off, b = (0, b + 8) if k < TILES - 1 else (1, 0)
        b -= 1 if off == 0 else 0
        for half in range(2):
            put(b + half, "pe", "turn_probs", off, k, half)
            put(b + half, "act", "copy_probs", off, k, half)
        put(b + 3, "pe", "attend", off, k)
        put(b + 3, "dve", "normalise", off, k)
    put(0, "sp", "load_ctx", 1)
    put(0, "sp", "load_x", 1)
    put(4, "pe", "v", 0)
    put(4, "act", "copy_v", 0)
    put(5, "sp", "load_xt", -1)
    put(3, "pool", "x_plus_bo", 1)
    put(5, "pe", "turn_o", 1)
    put(5, "act", "copy_ot", 1)
    put(6, "pe", "out_proj", 1)
    put(6, "dve", "ln1_stats", 1)
    put(6, "pool", "rstd", 1, 0)
    put(7, "dve", "ln1_apply", 1)
    put(8, "pe", "turn_x1", 1)
    put(8, "act", "x1t_high", 1)
    put(8, "dve", "x1t_low", 1)
    for b in range(UB):
        put(4 + b, "dve", "gate_sums", 1, b)
    put(13, "dve", "gate_scale", 1)
    put(13, "dve", "ln2_stats", 2)
    put(13, "pool", "rstd", 2, 1)
    put(15, "dve", "ln2_apply", 2)
    put(16, "pe", "turn_x2", 2)
    put(16, "act", "x2t_high", 2)
    put(16, "dve", "x2t_low", 2)
    put(17, "pe", "hadamard", 2)
    put(17, "dve", "quantise", 2)
    put(18, "act", "to_q4", 2)
    put(20, "pe", "turn_q4", 2)
    put(20, "act", "copy_q4t", 2)
    put(21, "pe", "ffn", 2)
    put(22, "dve", "ln3_stats", 2)
    put(22, "pool", "rstd", 2, 2)
    put(23, "dve", "ln3_apply", 2)
    put(23, "sp", "store", 2)
    put(19, "pe", "q", -1)
    put(19, "act", "copy_q", -1)
    put(22, "pe", "k", -1)
    put(22, "act", "copy_k", -1)
    for k in range(TILES):
        put(22 + k, "pool", "spread_q", -1, k)
    for e in range(EXPERTS):
        it, slot = divmod(PREP_SLOTS * e, SLOTS)
        if it == iteration:
            put(slot, "sp", "load_w", it, e)
            put(slot, "act", "w_squares", it, e)
            put(slot + 1, "pe", "w_sum", it, e)
            put(slot + 1, "dve", "w_scale", it, e)
            put(slot + 2, "act", "w_high", it, e)
            put(slot + 2, "dve", "w1_low", it, e)
            put(slot + 2, "pool", "w2_low", it, e)
    if iteration == 0:
        put(4, "act", "ffn_abs", 0)
        put(5, "pe", "ffn_sum", 0)
        put(6, "dve", "ffn_ternary", 0)
    return [x for slot in at for x in slot]


SCHEDULE = build_schedule(None)
FIRST_SCHEDULES = {0: build_schedule(0), 1: build_schedule(1)}
FIRST_LOOP, LAST_LOOP = 2, UNITS - 2
ITERATIONS = UNITS + 2


def decoder_layer(nc, x, xt, ctx_w, itok, wqt, bq, wkt, bk, wvt, bv, wot, bo, w1t, w2t, ffnt,
                  c_ident, c_hadamard, c_causal, c_heads, out):
    with ExitStack() as stack:
        def sb(name, shape, dt=F32):
            return stack.enter_context(nc.sbuf_tensor(name, shape, dt))

        def sem(name):
            return stack.enter_context(nc.semaphore(name))

        def bank(name):
            return stack.enter_context(nc.psum_tensor(name, [P, 512], F32))

        wq_sb, wk_sb, wv_sb, wo_sb = (sb(n, [P, CD, D]) for n in ("wq_sb", "wk_sb", "wv_sb", "wo_sb"))
        bq_sb, bk_sb, bv_sb = (sb(n, [P, CD]) for n in ("bq_sb", "bk_sb", "bv_sb"))
        bo_sb = sb("bo_sb", [P, D])
        w1_hi, w1_lo = (sb(n, [P, EXPERTS, CD, HIDDEN], F16) for n in ("w1_hi", "w1_lo"))
        w2_hi, w2_lo = (sb(n, [P, EXPERTS, CH, D], F16) for n in ("w2_hi", "w2_lo"))
        w1_raw = sb("w1_raw", [P, STAGED, CD, HIDDEN])
        w2_raw = sb("w2_raw", [P, STAGED, CH, D])
        w_sq = sb("w_sq", [P, EXPERTS, 2])
        w_ms = sb("w_ms", [P, EXPERTS, 2])
        w_half = sb("w_half", [P, EXPERTS, 2], I32)
        w_pow = sb("w_pow", [P, EXPERTS, 2])
        w_inv = sb("w_inv", [P, EXPERTS, 2])
        w_undo = sb("w_undo", [P, EXPERTS])
        had_sb = sb("had_sb", [P, CD, D])
        had_h = sb("had_h", [P, CD, D], F16)
        ffn_sb = sb("ffn_sb", [P, CD, D])
        tern_sb = sb("tern_sb", [P, CD, D], BF16)
        wscale = sb("wscale", [P, D])
        ident = sb("ident", [P, P])
        ident_h = sb("ident_h", [P, P], BF16)
        causal = sb("causal", [P, S_COLS])
        causal_h = sb("causal_h", [P, S_COLS], BF16)
        head_mask = sb("head_mask", [P, HG])
        ones = sb("ones", [P, P])
        minus_half = sb("minus_half", [P, UB])
        xt_sb = sb("xt_sb", [P, CD, UT])
        qt_sb = sb("qt_sb", [P, GROUPS, UT])
        kt_sb = sb("kt_sb", [P, GROUPS, UT])
        q_spread = sb("q_spread", [P, TILES, BLOCKS, HG, QB])
        v_sb = sb("v_sb", [P, UB * HEADS, VW])
        s_sb = sb("s_sb", [P, 2, S_COLS])
        top8 = sb("top8", [P, 2, BLOCKS, 8])
        next8 = sb("next8", [P, BLOCKS, 8])
        neg_max = sb("neg_max", [P, 2, BLOCKS])
        taken = sb("taken", [P, P_COLS])
        e_sb = sb("e_sb", [P, 2, P_COLS])
        p_sb = sb("p_sb", [P, 2, P_COLS])
        pt_sb = sb("pt_sb", [P, 2, HG, BLOCKS, QB])
        rsum = sb("rsum", [P, HG])
        o_sb = sb("o_sb", [P, UB, D])
        ot_sb = sb("ot_sb", [P, CD, UT])
        x_sb = sb("x_sb", [P, UB, D])
        xb_sb = sb("xb_sb", [P, UB, D])
        t1 = sb("t1", [P, UB, D])
        t3 = sb("t3", [P, UB, D])
        stats = sb("stats", [P, 3, UB, 6])
        meanvar = sb("meanvar", [P, 3, UB, 2])
        var_eps = sb("var_eps", [P, 3, UB])
        rstd = sb("rstd", [P, 3, UB])
        x1 = sb("x1", [P, UB, D])
        x1t_hi, x1t_lo = sb("x1t_hi", [P, CD, UT], F16), sb("x1t_lo", [P, CD, UT], F16)
        x2 = sb("x2", [P, UB, D])
        x2t_hi, x2t_lo = sb("x2t_hi", [P, CD, UT], F16), sb("x2t_lo", [P, CD, UT], F16)
        out_sb = sb("out_sb", [P, UB, D])
        ctx_sb = sb("ctx_sb", [P, UB, SEQ])
        itok_sb = sb("itok_sb", [P, UB, SEQ], I32)
        gate_part = sb("gate_part", [P, UB, EXPERTS, SEQ], BF16)
        gate_raw = sb("gate_raw", [P, UB, EXPERTS])
        gate = sb("gate", [P, UB, EXPERTS])
        h_raw = sb("h_raw", [P, 2, 2, UT])
        h_hi, h_lo = sb("h_hi", [P, 2, CH, UT], F16), sb("h_lo", [P, 2, CH, UT], F16)
        acc = sb("acc", [P, UB, D])
        amax = sb("amax", [P, UB])
        xscale = sb("xscale", [P, UB])
        xscale_inv = sb("xscale_inv", [P, UB])
        rounded = sb("rounded", [P, UB, D])
        clipped = sb("clipped", [P, UB, D])
        q4 = sb("q4", [P, UB, D], BF16)
        q4t = sb("q4t", [P, CD, UT], BF16)
        f_sb = sb("f_sb", [P, UB, D])
        tmp_a, tmp_b = rounded, clipped

        ps_hi, ps_lo, ps_pt, ps_misc = bank("ps_hi"), bank("ps_lo"), bank("ps_pt"), bank("ps_misc")
        ps_z = [bank("ps_z0"), bank("ps_z1")]
        ps_o = [bank("ps_o0"), bank("ps_o1")]
        misc_h = ps_misc[:, :].bitcast(BF16)

        s_const, s_qk, s_vo, s_ffnw = sem("s_const"), sem("s_qk"), sem("s_vo"), sem("s_ffnw")
        w_loaded = [sem(f"w_loaded{i}") for i in range(STAGED)]
        w_squared, w_summed, w_step, w_high_ready, w_low_step, w2_low_ready, w_undo_step, had_cast = (
            sem(n) for n in ("w_squared", "w_summed", "w_step", "w_high_ready", "w_low_step", "w2_low_ready",
                             "w_undo_step", "had_cast"))
        s_xt, s_x, s_ctx, s_store = sem("xt_loaded"), sem("x_loaded"), sem("ctx_loaded"), sem("out_stored")
        zeroed, pool_const, cast_done, ffn_prep, ffn_abs, ffn_sum = (
            sem("zeroed"), sem("pool_const"), sem("cast_done"), sem("ffn_prep"), sem("ffn_abs"), sem("ffn_sum"))
        q_ready, k_ready, v_ready, s_ready, pt_ready, pv_ready = (
            sem(n) for n in ("q_ready", "k_ready", "v_ready", "s_ready", "pt_ready", "pv_ready"))
        ot_ready, y_ready, x1t_ready, l1_done, l2_done = (
            sem(n) for n in ("ot_ready", "y_ready", "x1t_ready", "l1_done", "l2_done"))
        x2t_ready, xh_ready, q4t_ready, f_ready = (
            sem(n) for n in ("x2t_ready", "xh_ready", "q4t_ready", "f_ready"))
        q_copied, k_copied, v_copied, s_copied, pt_copied, ot_copied = (
            sem(n) for n in ("q_copied", "k_copied", "v_copied", "s_copied", "pt_copied", "ot_copied"))
        x1t_high, x2t_high, q4t_copied, relu_done, e_ready, q4_ready = (
            sem(n) for n in ("x1t_high", "x2t_high", "q4t_copied", "relu_done", "e_ready", "q4_ready"))
        x1t_low, x2t_low, w1_low_ready = sem("x1t_low"), sem("x2t_low"), sem("w1_low_ready")
        max_ready, nmax_ready, sel_step, p_ready, rsum_ready, o_ready = (
            sem(n) for n in ("max_ready", "nmax_ready", "sel_step", "p_ready", "rsum_ready", "o_ready"))
        t1_ready, t3_ready, gate_summed, gate_ready, acc_done, x1_ready, x2_ready, out_ready = (
            sem(n) for n in ("t1_ready", "t3_ready", "gate_summed", "gate_ready", "acc_done", "x1_ready",
                             "x2_ready", "out_ready"))
        stat_step = [sem(f"stat_step{i}") for i in range(3)]
        dve_held, pool_held = sem("dve_held"), sem("pool_held")
        quant_step, inv_ready, f_scaled = sem("quant_step"), sem("inv_ready"), sem("f_scaled")
        spread_ready, xb_ready, h_low_done = sem("spread_ready"), sem("xb_ready"), sem("h_low_done")
        eps_added = [sem(f"eps_added{i}") for i in range(3)]
        rstd_ready = [sem(f"rstd_ready{i}") for i in range(3)]

        MISC = {
            "q": (q_copied, 1, lambda k: 1), "k": (k_copied, 1, lambda k: 1), "v": (v_copied, 1, lambda k: 1),
            "attend": (o_ready, TILES, lambda k: k + 1), "turn_o": (ot_copied, 1, lambda k: 1),
            "out_proj": (t1_ready, 1, lambda k: 1), "turn_x1": (x1t_low, 1, lambda k: 1),
            "turn_x2": (x2t_low, 1, lambda k: 1),
            "hadamard": (quant_step, 4, lambda k: 3), "turn_q4": (q4t_copied, 1, lambda k: 1),
            "ffn": (f_scaled, 1, lambda k: 1),
        }

        def walk(engine, step, eng):
            def iteration(u, inside):
                for e, name, off, args in (SCHEDULE if inside else FIRST_SCHEDULES.get(u, SCHEDULE)):
                    if e == engine and (inside or 0 <= u - off < UNITS):
                        step(name, u - off, off, *args)
            for u in range(-1, FIRST_LOOP):
                iteration(u, False)
            with eng.Fori(FIRST_LOOP, LAST_LOOP + 1) as u:
                iteration(u, True)
            for u in range(LAST_LOOP + 1, ITERATIONS):
                iteration(u, False)

        def wait(eng, s, value):
            if not isinstance(value, int) or value > 0:
                eng.wait_ge(s, value)

        block = stack.enter_context(nc.Block())

        @block.sync
        def _(sp):
            def rows(a):
                return a.rearrange("(c p) n -> p c n", p=P)

            def load_xt(v):
                wait(sp, v_ready, v)
                sp.dma_start(xt_sb[:, :, :], rows(xt)[:, :, bass.ds(v * UT, UT)]).then_inc(s_xt, 16)

            def step(name, v, off, *args):
                if name == "load_xt":
                    if not isinstance(v, int) or v > 0:
                        load_xt(v)
                elif name == "load_x":
                    wait(sp, xb_ready, v)
                    sp.dma_start(x_sb[:, :, :], x.rearrange("b s d -> s b d")[:, bass.ds(v * UB, UB), :])\
                        .then_inc(s_x, 16)
                elif name == "load_ctx":
                    wait(sp, gate_summed, UB * v)
                    sp.dma_start(ctx_sb[:, :, :], ctx_w.rearrange("b s k -> s b k")[:, bass.ds(v * UB, UB), :])\
                        .then_inc(s_ctx, 16)
                    sp.dma_start(itok_sb[:, :, :], itok.rearrange("b s k -> s b k")[:, bass.ds(v * UB, UB), :])\
                        .then_inc(s_ctx, 16)
                elif name == "load_w":
                    e, = args
                    wait(sp, w1_low_ready, e - STAGED + 1)
                    wait(sp, w2_low_ready, e - STAGED + 1)
                    sp.dma_start(w1_raw[:, e % STAGED, :, :], rows(w1t[e])).then_inc(w_loaded[e % STAGED], 16)
                    sp.dma_start(w2_raw[:, e % STAGED, :, :], rows(w2t[e])).then_inc(w_loaded[e % STAGED], 16)
                elif name == "store":
                    sp.wait_ge(out_ready, v + 1)
                    sp.dma_start(out.rearrange("b s d -> s b d")[:, bass.ds(v * UB, UB), :], out_sb[:, :, :])\
                        .then_inc(s_store, 16)

            sp.dma_start(wq_sb[:, :, :], rows(wqt)).then_inc(s_qk, 16)
            load_xt(0)
            sp.dma_start(wk_sb[:, :, :], rows(wkt)).then_inc(s_qk, 16)
            for dst, src in ((bq_sb, bq), (bk_sb, bk), (head_mask, c_heads), (causal, c_causal), (ident, c_ident)):
                sp.dma_start(dst[:, :], src[:, :]).then_inc(s_const, 16)
            sp.dma_start(wv_sb[:, :, :], rows(wvt)).then_inc(s_vo, 16)
            sp.dma_start(ffn_sb[:, :, :], rows(ffnt)).then_inc(s_ffnw, 16)
            sp.dma_start(had_sb[:, :, :], rows(c_hadamard)).then_inc(s_ffnw, 16)
            sp.dma_start(wo_sb[:, :, :], rows(wot)).then_inc(s_vo, 16)
            sp.dma_start(bv_sb[:, :], bv[:, :]).then_inc(s_vo, 16)
            sp.dma_start(bo_sb[:, :], bo.rearrange("(a n) -> a n", a=1).broadcast_to([P, D])).then_inc(s_vo, 16)
            sp.sem_inc(s_store, 16)
            walk("sp", step, sp)
            sp.wait_ge(s_store, 16 * (UNITS + 1))

        CONSTS = 5 * 16

        @block.gpsimd
        def _(pool):
            nc.gpsimd.memset(minus_half[:, :], -0.5)
            nc.gpsimd.memset(ones[:, :], 1.0)
            nc.gpsimd.memset(v_sb[:, :, DH:VW], 1.0)
            nc.gpsimd.memset(pt_sb[:, :, :, :, :], 0.0).then_inc(pool_const, 1)
            pool.wait_ge(s_const, CONSTS)

            def step(name, v, off, *args):
                if name == "spread_q":
                    k, = args
                    b, g = divmod(k, GROUPS)
                    pool.wait_ge(q_copied, v + 1)
                    wait(pool, s_ready, 2 * (TILES * (v - 1) + k) + 2)
                    q_in = qt_sb[:, g, b * SEQ:(b + 1) * SEQ].rearrange("p (j a q) -> p j a q", a=1, q=QB)
                    nc.gpsimd.tensor_tensor(
                        q_spread[:, k, :, :, :], q_in.broadcast_to([P, BLOCKS, HG, QB]),
                        head_mask[:, :].rearrange("p (a h c) -> p a h c", a=1, c=1).broadcast_to([P, BLOCKS, HG, QB]),
                        ALU.mult).then_inc(spread_ready, 1)
                elif name == "x_plus_bo":
                    pool.wait_ge(s_x, 16 * (v + 1))
                    if isinstance(v, int) and v == 0:
                        pool.wait_ge(s_vo, 64)
                    wait(pool, t1_ready, v)
                    for b in range(UB):
                        last = nc.gpsimd.tensor_tensor(xb_sb[:, b, :], x_sb[:, b, :], bo_sb[:, :], ALU.add)
                    last.then_inc(xb_ready, 1)
                elif name == "h_low":
                    e, z = args
                    i = RING_STEPS * v + 2 * e + z
                    pool.wait_ge(relu_done, 2 * i + 2)
                    wait(pool, l2_done, RING_STEPS * v + 2 * e - 2)
                    nc.gpsimd.tensor_tensor(h_lo[:, e % 2, 2 * z:2 * z + 2, :], h_raw[:, z, :, :],
                                            h_hi[:, e % 2, 2 * z:2 * z + 2, :], ALU.subtract)\
                        .then_inc(h_low_done, 1)
                elif name == "w2_low":
                    e, = args
                    raw, hi = w2_raw[:, e % STAGED, :, :], w2_hi[:, e, :, :]
                    pool.wait_ge(w_high_ready, e + 1)
                    nc.gpsimd.tensor_scalar(raw, raw, w_pow[:, e, 1:2], 1.0, ALU.mult, ALU.mult)\
                        .then_inc(w_low_step, 1)
                    pool.wait_ge(w_low_step, e + 1)
                    nc.gpsimd.tensor_tensor(w2_lo[:, e, :, :], raw, hi, ALU.subtract).then_inc(w2_low_ready, 1)
                elif name == "rstd":
                    i, = args
                    pool.wait_ge(stat_step[i], 2 * (v + 1))
                    pool.sem_inc(pool_held, 1)
                    nc.gpsimd.tensor_scalar(var_eps[:, i, :], meanvar[:, i, :, 1], EPS, None, ALU.add)\
                        .then_inc(eps_added[i], 1)
                    pool.wait_ge(eps_added[i], v + 1)
                    nc.gpsimd.tensor_tensor(rstd[:, i, :], var_eps[:, i, :], minus_half[:, :], ALU.pow)\
                        .then_inc(rstd_ready[i], 1)

            walk("pool", step, pool)

        @block.scalar
        def _(act):
            act.wait_ge(s_const, CONSTS)
            act.activation(ident_h[:, :], ident[:, :], ACT.Copy)
            act.activation(causal_h[:, :], causal[:, :], ACT.Copy).then_inc(cast_done, 1)

            def step(name, v, off, *args):
                n = TILES * v + args[0] if name in ("exp", "copy_scores", "copy_probs") else None
                if name == "copy_q" or name == "copy_k":
                    ready, dst, bias, copied = ((q_ready, qt_sb, bq_sb, q_copied) if name == "copy_q"
                                                else (k_ready, kt_sb, bk_sb, k_copied))
                    act.wait_ge(ready, v + 1)
                    if name == "copy_q":
                        wait(act, spread_ready, TILES * v)
                    for g in range(GROUPS):
                        last = act.activation(dst[:, g, :], ps_misc[:, g * UT:(g + 1) * UT], ACT.Identity,
                                              bias=bias[:, g:g + 1])
                    last.then_inc(copied, 1)
                elif name == "copy_v":
                    act.wait_ge(v_ready, v + 1)
                    act.activation(v_sb[:, :, 0:DH], ps_misc[:, :].rearrange("p (h d) -> p h d", d=DH), ACT.Copy)\
                        .then_inc(v_copied, 1)
                elif name == "copy_scores":
                    k, = args
                    wait(act, p_ready, n - 1)
                    act.wait_ge(s_ready, 2 * n + 1)
                    act.activation(s_sb[:, k % 2, block_at(HALF):S_COLS], ps_hi[:, 0:S_COLS - block_at(HALF)],
                                   ACT.Copy).then_inc(s_copied, 1)
                    act.wait_ge(s_ready, 2 * n + 2)
                    act.activation(s_sb[:, k % 2, 0:block_at(HALF)], ps_lo[:, 0:block_at(HALF)],
                                   ACT.Copy).then_inc(s_copied, 1)
                elif name == "exp":
                    k, = args
                    act.wait_ge(nmax_ready, n + 1)
                    wait(act, p_ready, n - 1)
                    wait(act, pt_ready, 2 * n - 2)
                    for j in range(BLOCKS):
                        m = QB * (j + 1)
                        dst = p_sb if j < FREE_BLOCKS else e_sb
                        last = act.activation(dst[:, k % 2, prob_at(j):prob_at(j) + m],
                                              s_sb[:, k % 2, block_at(j):block_at(j) + m], ACT.Exp,
                                              bias=neg_max[:, k % 2, j:j + 1], scale=SCALE)
                    last.then_inc(e_ready, 1)
                elif name == "copy_probs":
                    k, half = args
                    rows = P if half else P // 2
                    act.wait_ge(pt_ready, 2 * n + half + 1)
                    wait(act, pv_ready, n - 1)
                    act.activation(
                        pt_sb[0:rows, k % 2, :, HALF * half:HALF * (half + 1), :].rearrange("p h j q -> p j h q"),
                        ps_pt[0:rows, :].rearrange("p (j h q) -> p j h q", h=HG, q=QB), ACT.Copy)\
                        .then_inc(pt_copied, 1)
                elif name == "copy_ot":
                    act.wait_ge(ot_ready, v + 1)
                    if isinstance(v, int) and v == 0:
                        act.wait_ge(s_vo, 64)
                    for c in range(CD):
                        last = act.activation(ot_sb[:, c, :], ps_misc[:, c * UT:(c + 1) * UT], ACT.Identity,
                                              bias=bv_sb[:, c:c + 1])
                    last.then_inc(ot_copied, 1)
                elif name in ("x1t_high", "x2t_high"):
                    ready, dst, done = ((x1t_ready, x1t_hi, x1t_high) if name == "x1t_high"
                                        else (x2t_ready, x2t_hi, x2t_high))
                    act.wait_ge(ready, v + 1)
                    act.activation(dst[:, :, :], ps_misc[:, :].rearrange("p (c t) -> p c t", c=CD), ACT.Copy)\
                        .then_inc(done, 1)
                elif name == "relu":
                    e, z = args
                    i = RING_STEPS * v + 2 * e + z
                    act.wait_ge(l1_done, i + 1)
                    wait(act, l2_done, RING_STEPS * v + 2 * e - 2)
                    act.activation(h_hi[:, e % 2, 2 * z:2 * z + 2, :],
                                   ps_z[z][:, :].rearrange("p (c t) -> p c t", c=2), ACT.Relu)\
                        .then_inc(relu_done, 1)
                    wait(act, h_low_done, i - 1)
                    act.activation(h_raw[:, z, :, :],
                                   ps_z[z][:, :].rearrange("p (c t) -> p c t", c=2), ACT.Relu)\
                        .then_inc(relu_done, 1)
                elif name == "ffn_abs":
                    act.wait_ge(s_ffnw, 32)
                    act.activation(tmp_a[:, :, :], ffn_sb[:, :, :], ACT.Abs).then_inc(ffn_abs, 1)
                    act.activation(had_h[:, :, :], had_sb[:, :, :], ACT.Copy).then_inc(had_cast, 1)
                elif name == "w_squares":
                    e, = args
                    act.wait_ge(w_loaded[e % STAGED], 32 * (e // STAGED + 1))
                    act.activation(w1_hi[:, e, :, :], w1_raw[:, e % STAGED, :, :], ACT.Square,
                                   accum_out=w_sq[:, e, 0:1])
                    act.activation(w2_hi[:, e, :, :], w2_raw[:, e % STAGED, :, :], ACT.Square,
                                   accum_out=w_sq[:, e, 1:2]).then_inc(w_squared, 1)
                elif name == "w_high":
                    e, = args
                    act.wait_ge(w_step, 3 * (e + 1))
                    act.activation(w1_hi[:, e, :, :], w1_raw[:, e % STAGED, :, :], ACT.Copy,
                                   scale=w_pow[:, e, 0:1])
                    act.activation(w2_hi[:, e, :, :], w2_raw[:, e % STAGED, :, :], ACT.Copy,
                                   scale=w_pow[:, e, 1:2]).then_inc(w_high_ready, 1)
                elif name == "to_q4":
                    act.wait_ge(quant_step, 4 * (v + 1))
                    act.activation(q4[:, :, :], clipped[:, :, :], ACT.Copy, bias=-ROUND).then_inc(q4_ready, 1)
                elif name == "copy_q4t":
                    act.wait_ge(q4t_ready, v + 1)
                    act.activation(q4t[:, :, :], misc_h[:, 0:CD * UT].rearrange("p (c t) -> p c t", c=CD), ACT.Copy)\
                        .then_inc(q4t_copied, 1)

            walk("act", step, act)

        @block.tensor
        def _(pe):
            misc_before = [None]

            def take_misc(name, v, off, k=0):
                if misc_before[0] is not None:
                    s, per_unit, count, v0, off0, k0 = misc_before[0]
                    if not isinstance(v, int) and isinstance(v0, int):
                        v0 = v + (off - off0 - 1)
                    elif isinstance(v, int) and not isinstance(v0, int):
                        v0 = LAST_LOOP - off0
                    pe.wait_ge(s, v0 * per_unit + count(k0))
                misc_before[0] = (*MISC[name], v, off, k)

            def project(w, ready):
                for g in range(GROUPS):
                    for c in range(CD):
                        last = pe.matmul(ps_misc[:, g * UT:(g + 1) * UT], w[:, c, g * P:(g + 1) * P],
                                         xt_sb[:, c, :], start=c == 0, stop=c == CD - 1)
                last.then_inc(ready, 1)

            def rows_by(lhs_parts, rhs, ready):
                terms = [(lhs, c) for c in range(CD) for lhs in lhs_parts]
                for b in range(UB):
                    for n, (lhs, c) in enumerate(terms):
                        last = pe.matmul(ps_misc[:, b * D:(b + 1) * D], lhs[:, c, b * SEQ:(b + 1) * SEQ],
                                         rhs[:, c, :], start=n == 0, stop=n == len(terms) - 1)
                last.then_inc(ready, 1)

            def turn(src, idn, ready, dst):
                for c in range(CD):
                    for b in range(UB):
                        last = pe.transpose(dst[:, c * UT + b * SEQ:c * UT + (b + 1) * SEQ],
                                            src[:, b, c * P:(c + 1) * P], idn[:, :])
                last.then_inc(ready, 1)

            def step(name, v, off, *args):
                if name in MISC:
                    take_misc(name, v, off, *args)
                if name == "q":
                    pe.wait_ge(s_xt, 16 * (v + 1))
                    project(wq_sb, q_ready)
                elif name == "k":
                    project(wk_sb, k_ready)
                elif name == "v":
                    if off == 0 and isinstance(v, int) and v == 0:
                        pe.wait_ge(s_vo, 64)
                    rows_by([xt_sb], wv_sb, v_ready)
                elif name == "ffn_sum":
                    pe.wait_ge(pool_const, 1)
                    pe.wait_ge(ffn_abs, 1)
                    for c in range(CD):
                        last = pe.matmul(ps_o[1][:, 0:D], ones[:, :], tmp_a[:, c, :], start=c == 0, stop=c == CD - 1)
                    last.then_inc(ffn_sum, 1)
                elif name == "scores":
                    k, = args
                    n = TILES * v + k
                    b, g = divmod(k, GROUPS)
                    if k == 0 and isinstance(v, int) and v == 0:
                        pe.wait_ge(cast_done, 1)
                    pe.wait_ge(spread_ready, n + 1)
                    pe.wait_ge(k_copied, v + 1)
                    for half, ps in ((1, ps_hi), (0, ps_lo)):
                        wait(pe, s_copied, 2 * n - half)
                        base, end = block_at(HALF * half), block_at(HALF * (half + 1))
                        pe.matmul(ps[:, 0:end - base], ident_h[:, :], causal_h[:, base:end], start=True, stop=True,
                                  skip_group_check=True)
                        for j in range(HALF * half, HALF * (half + 1)):
                            m, at = QB * (j + 1), block_at(j) - base
                            last = pe.matmul(ps[:, at:at + m],
                                             q_spread[:, k, j, :, :].rearrange("p h q -> p (h q)"),
                                             kt_sb[:, g, b * SEQ:b * SEQ + m], start=False,
                                             stop=True, skip_group_check=True)
                        last.then_inc(s_ready, 1)
                elif name == "turn_probs":
                    k, half = args
                    n = TILES * v + k
                    pe.wait_ge(p_ready, n + 1)
                    wait(pe, pt_copied, 2 * n + half)
                    for i in range(HALF):
                        at = prob_at(HALF * half + i)
                        last = pe.transpose(ps_pt[:, i * P:(i + 1) * P], p_sb[:, k % 2, at:at + P], ident[:, :])
                    last.then_inc(pt_ready, 1)
                elif name == "attend":
                    k, = args
                    n = TILES * v + k
                    b, g = divmod(k, GROUPS)
                    pe.wait_ge(pt_copied, 2 * n + 2)
                    pe.wait_ge(v_copied, v + 1)
                    for h in range(HG):
                        last = pe.matmul(ps_misc[:, h * VW:(h + 1) * VW], pt_sb[:, k % 2, h, :, :].rearrange("p j q -> p (j q)"),
                                         v_sb[:, b * HEADS + g * HG + h, :], start=True, stop=True)
                    last.then_inc(pv_ready, 1)
                elif name == "turn_o":
                    pe.wait_ge(o_ready, TILES * (v + 1))
                    turn(o_sb, ident, ot_ready, ps_misc)
                elif name == "out_proj":
                    pe.wait_ge(ot_copied, v + 1)
                    rows_by([ot_sb], wo_sb, y_ready)
                elif name == "turn_x1":
                    pe.wait_ge(x1_ready, v + 1)
                    turn(x1, ident, x1t_ready, ps_misc)
                elif name == "L1":
                    e, z = args
                    i = RING_STEPS * v + 2 * e + z
                    if e == 0 and z == 0:
                        pe.wait_ge(x1t_low, v + 1)
                    if off == 2 or isinstance(v, int):
                        pe.wait_ge(w1_low_ready, e + 1)
                    wait(pe, relu_done, 2 * i - 2)
                    for d in range(2):
                        at = (2 * z + d) * P
                        terms = [(w, x, c) for c in range(CD) for w, x in ((w1_lo, x1t_hi), (w1_hi, x1t_lo),
                                                                           (w1_hi, x1t_hi))]
                        for n, (w, x, c) in enumerate(terms):
                            last = pe.matmul(ps_z[z][:, d * UT:(d + 1) * UT], w[:, e, c, at:at + P], x[:, c, :],
                                             start=n == 0, stop=n == len(terms) - 1)
                    last.then_inc(l1_done, 1)
                elif name == "L2":
                    e, b = args
                    i = RING_STEPS * v + 2 * e + b
                    if off == 2 or isinstance(v, int):
                        pe.wait_ge(w2_low_ready, e + 1)
                    pe.wait_ge(h_low_done, RING_STEPS * v + 2 * e + 2)
                    wait(pe, acc_done, i - 1)
                    if isinstance(v, int) and v == 0 and e == 0:
                        pe.wait_ge(*((w_step, 3 * EXPERTS - 2), (ffn_prep, 1))[b])
                    terms = [(h, w, c) for c in range(CH) for h, w in ((h_lo, w2_hi), (h_hi, w2_lo), (h_hi, w2_hi))]
                    for n, (h, w, c) in enumerate(terms):
                        last = pe.matmul(ps_o[b][:, 0:D], h[:, e % 2, c, b * SEQ:(b + 1) * SEQ], w[:, e, c, :],
                                         start=n == 0, stop=n == len(terms) - 1)
                    last.then_inc(l2_done, 1)
                elif name == "w_sum":
                    e, = args
                    pe.wait_ge(w_squared, e + 1)
                    wait(pe, w_step, 3 * e - 2)
                    pe.matmul(ps_o[0][:, 0:2], ones[:, :], w_sq[:, e, :], start=True, stop=True)\
                        .then_inc(w_summed, 1)
                elif name == "turn_x2":
                    pe.wait_ge(x2_ready, v + 1)
                    turn(x2, ident, x2t_ready, ps_misc)
                elif name == "hadamard":
                    pe.wait_ge(x2t_low, v + 1)
                    pe.wait_ge(had_cast, 1)
                    rows_by([x2t_lo, x2t_hi], had_h, xh_ready)
                elif name == "turn_q4":
                    pe.wait_ge(q4_ready, v + 1)
                    turn(q4, ident_h, q4t_ready, misc_h)
                elif name == "ffn":
                    pe.wait_ge(q4t_copied, v + 1)
                    pe.wait_ge(ffn_prep, 3)
                    rows_by([q4t], tern_sb, f_ready)

            pe.wait_ge(s_qk, 32)
            walk("pe", step, pe)

        @block.vector
        def _(dve):
            V = nc.vector

            def layernorm_stats(i, src, v):
                for b in range(UB):
                    last = V.bn_stats(stats[:, i, b, :], src[:, b, :])
                last.then_inc(stat_step[i], 1)
                dve.wait_ge(stat_step[i], 2 * v + 1)
                dve.sem_inc(dve_held, 1)
                for b in range(UB):
                    last = V.bn_aggr(meanvar[:, i, b, :], stats[:, i, b, :])
                last.then_inc(stat_step[i], 1)

            def layernorm_apply(i, dst, src, v, ready):
                dve.wait_ge(rstd_ready[i], v + 1)
                for b in range(UB):
                    last = V.tensor_scalar(dst[:, b, :], src[:, b, :], meanvar[:, i, b, 0:1], rstd[:, i, b:b + 1],
                                           ALU.subtract, ALU.mult)
                last.then_inc(ready, 1)

            def step(name, v, off, *args):
                if name == "first_max":
                    k, = args
                    n = TILES * v + k
                    dve.wait_ge(s_copied, 2 * n + 2)
                    wait(dve, e_ready, n - 1)
                    dve.sem_inc(dve_held, 1)
                    for j in range(BLOCKS):
                        last = V.max(top8[:, k % 2, j, :], s_sb[:, k % 2, block_at(j):block_at(j + 1)])
                    last.then_inc(max_ready, 1)
                    dve.wait_ge(max_ready, n + 1)
                    V.tensor_scalar(neg_max[:, k % 2, :], top8[:, k % 2, :, 0], -SCALE, None, ALU.mult)\
                        .then_inc(nmax_ready, 1)
                elif name == "select":
                    k, r = args
                    n = TILES * v + k
                    if r == 0:
                        wait(dve, p_ready, n)
                    for i, j in enumerate(range(FREE_BLOCKS, BLOCKS)):
                        m = QB * (j + 1)
                        t = taken[:, prob_at(j):prob_at(j) + m]
                        if r > 0 and i % SEL_GROUP == 0:
                            dve.wait_ge(sel_step, SEL_STEPS * n + 2 * (r - 1) + i // SEL_GROUP + 1)
                        if i % SEL_GROUP == 0:
                            dve.sem_inc(dve_held, 1)
                        if r % 2 == 1:
                            last = V.max(next8[:, j, :], t)
                        elif r == 0:
                            last = V.match_replace(t, top8[:, k % 2, j, :],
                                                   s_sb[:, k % 2, block_at(j):block_at(j) + m], TAKEN)
                        else:
                            last = V.match_replace(t, next8[:, j, :], t, TAKEN)
                        if i % SEL_GROUP == SEL_GROUP - 1:
                            last.then_inc(sel_step, 1)
                elif name == "keep":
                    k, = args
                    n = TILES * v + k
                    dve.wait_ge(e_ready, n + 1)
                    dve.wait_ge(sel_step, SEL_STEPS * (n + 1))
                    wait(dve, pt_ready, 2 * n - 2)
                    V.scalar_tensor_tensor(p_sb[:, k % 2, SEL_FROM:P_COLS], taken[:, SEL_FROM:P_COLS], TAKEN,
                                           e_sb[:, k % 2, SEL_FROM:P_COLS], ALU.is_equal, ALU.mult)\
                        .then_inc(p_ready, 1)
                elif name == "normalise":
                    k, = args
                    n = TILES * v + k
                    b, g = divmod(k, GROUPS)
                    dve.wait_ge(pv_ready, n + 1)
                    wait(dve, ot_ready, v)
                    pv = ps_misc[:, 0:HG * VW].rearrange("p (h c) -> p h c", c=VW)
                    V.reciprocal(rsum[:, :], pv[:, :, DH]).then_inc(rsum_ready, 1)
                    dve.wait_ge(rsum_ready, n + 1)
                    V.tensor_tensor(o_sb[:, b, g * P:(g + 1) * P].rearrange("p (h c) -> p h c", c=DH),
                                    pv[:, :, 0:DH],
                                    rsum[:, :].rearrange("p (h a) -> p h a", a=1).broadcast_to([P, HG, DH]),
                                    ALU.mult).then_inc(o_ready, 1)
                elif name == "ln1_stats":
                    dve.wait_ge(y_ready, v + 1)
                    dve.wait_ge(xb_ready, v + 1)
                    V.tensor_tensor(t1[:, :, :], ps_misc[:, :].rearrange("p (b n) -> p b n", b=UB),
                                    xb_sb[:, :, :], ALU.add).then_inc(t1_ready, 1)
                    dve.wait_ge(t1_ready, v + 1)
                    layernorm_stats(0, t1, v)
                elif name == "ln1_apply":
                    layernorm_apply(0, x1, t1, v, x1_ready)
                elif name == "gate_sums":
                    b, = args
                    dve.wait_ge(s_ctx, 32 * (v + 1))
                    for e in range(EXPERTS):
                        last = V.scalar_tensor_tensor(gate_part[:, b, e, :], itok_sb[:, b, :], float(e),
                                                      ctx_sb[:, b, :], ALU.is_equal, ALU.mult,
                                                      accum_out=gate_raw[:, b, e:e + 1])
                    last.then_inc(gate_summed, 1)
                elif name == "gate_scale":
                    dve.wait_ge(gate_summed, UB * (v + 1))
                    dve.wait_ge(w_undo_step, 2)
                    wait(dve, acc_done, RING_STEPS * v)
                    undo = w_undo[:, :].rearrange("p (b e) -> p b e", b=1).broadcast_to([P, UB, EXPERTS])
                    V.tensor_tensor(gate[:, :, :], gate_raw[:, :, :], undo, ALU.mult).then_inc(gate_ready, 1)
                elif name in ("x1t_low", "x2t_low"):
                    high, hi, lo, done = ((x1t_high, x1t_hi, x1t_lo, x1t_low) if name == "x1t_low"
                                          else (x2t_high, x2t_hi, x2t_lo, x2t_low))
                    dve.wait_ge(high, v + 1)
                    V.tensor_tensor(lo[:, :, :], ps_misc[:, :].rearrange("p (c t) -> p c t", c=CD), hi[:, :, :],
                                    ALU.subtract).then_inc(done, 1)
                elif name == "ffn_ternary":
                    dve.wait_ge(ffn_sum, 1)
                    V.tensor_scalar(wscale[:, :], ps_o[1][:, 0:D], 1.0 / D, 1e-5, ALU.mult, ALU.max)\
                        .then_inc(ffn_prep, 1)
                    dve.wait_ge(ffn_prep, 1)
                    for c in range(CD):
                        V.scalar_tensor_tensor(tmp_a[:, c, :], wscale[:, :], 0.5, ffn_sb[:, c, :], ALU.mult,
                                               ALU.is_lt)
                        last = V.scalar_tensor_tensor(tmp_b[:, c, :], wscale[:, :], -0.5, ffn_sb[:, c, :], ALU.mult,
                                                      ALU.is_gt)
                    last.then_inc(ffn_prep, 1)
                    dve.wait_ge(ffn_prep, 2)
                    V.tensor_tensor(tern_sb[:, :, :], tmp_a[:, :, :], tmp_b[:, :, :], ALU.subtract)\
                        .then_inc(ffn_prep, 1)
                elif name == "w1_low":
                    e, = args
                    dve.wait_ge(w_high_ready, e + 1)
                    for c in range(CD):
                        last = V.scalar_tensor_tensor(w1_lo[:, e, c, :], w1_raw[:, e % STAGED, c, :],
                                                      w_pow[:, e, 0:1], w1_hi[:, e, c, :], ALU.mult, ALU.subtract)
                    last.then_inc(w1_low_ready, 1)
                elif name == "w_scale":
                    e, = args
                    dve.wait_ge(w_summed, e + 1)
                    V.tensor_scalar(w_ms[:, e, :], ps_o[0][:, 0:2], 1.0 / (HIDDEN * D), 1e-36, ALU.mult, ALU.max)\
                        .then_inc(w_step, 1)
                    dve.wait_ge(w_step, 3 * e + 1)
                    V.tensor_scalar(w_half[:, e, :], w_ms[:, e, :].bitcast(I32), 24, None, ALU.logical_shift_right)\
                        .then_inc(w_step, 1)
                    dve.wait_ge(w_step, 3 * e + 2)
                    V.tensor_scalar(w_pow[:, e, :].bitcast(I32), w_half[:, e, :], -float(EXPONENT),
                                    190.0 * EXPONENT, ALU.mult, ALU.add).then_inc(w_step, 1)
                    if e == EXPERTS - 1:
                        dve.wait_ge(w_step, 3 * EXPERTS)
                        V.tensor_scalar(w_inv[:, :, :].bitcast(I32), w_pow[:, :, :].bitcast(I32), -1.0,
                                        254.0 * EXPONENT, ALU.mult, ALU.add).then_inc(w_undo_step, 1)
                        dve.wait_ge(w_undo_step, 1)
                        V.tensor_tensor(w_undo[:, :], w_inv[:, :, 0], w_inv[:, :, 1], ALU.mult)\
                            .then_inc(w_undo_step, 1)
                elif name == "gated_sum":
                    e, b = args
                    i = RING_STEPS * v + 2 * e + b
                    dve.wait_ge(l2_done, i + 1)
                    if e == 0:
                        dve.wait_ge(gate_ready, v + 1)
                        wait(dve, x2_ready, v)
                    else:
                        dve.wait_ge(acc_done, i - 1)
                    prev = x1 if e == 0 else acc
                    V.scalar_tensor_tensor(acc[:, b, :], ps_o[b][:, 0:D], gate[:, b, e:e + 1], prev[:, b, :],
                                           ALU.mult, ALU.add).then_inc(acc_done, 1)
                elif name == "ln2_stats":
                    dve.wait_ge(acc_done, RING_STEPS * (v + 1))
                    layernorm_stats(1, acc, v)
                elif name == "ln2_apply":
                    layernorm_apply(1, x2, acc, v, x2_ready)
                elif name == "quantise":
                    dve.wait_ge(xh_ready, v + 1)
                    xh = ps_misc[:, :].rearrange("p (b n) -> p b n", b=UB)
                    V.tensor_reduce(amax[:, :], xh, AX_X, ALU.max, apply_absolute_value=True)\
                        .then_inc(quant_step, 1)
                    dve.wait_ge(quant_step, 4 * v + 1)
                    V.tensor_scalar(xscale[:, :], amax[:, :], 1e-5, 1.0 / QPOS, ALU.max, ALU.mult)\
                        .then_inc(quant_step, 1)
                    dve.wait_ge(quant_step, 4 * v + 2)
                    V.reciprocal(xscale_inv[:, :], xscale[:, :]).then_inc(inv_ready, 1)
                    dve.wait_ge(inv_ready, v + 1)
                    for b in range(UB):
                        last = V.tensor_scalar(rounded[:, b, :], xh[:, b, :], xscale_inv[:, b:b + 1], ROUND,
                                               ALU.mult, ALU.add)
                    last.then_inc(quant_step, 1)
                    dve.wait_ge(quant_step, 4 * v + 3)
                    V.tensor_scalar(clipped[:, :, :], rounded[:, :, :], ROUND - QNEG, ROUND + QPOS, ALU.max,
                                    ALU.min).then_inc(quant_step, 1)
                elif name == "ln3_stats":
                    dve.wait_ge(f_ready, v + 1)
                    for b in range(UB):
                        last = V.scalar_tensor_tensor(f_sb[:, b, :], ps_misc[:, b * D:(b + 1) * D],
                                                      xscale[:, b:b + 1], wscale[:, :], ALU.mult, ALU.mult)
                    last.then_inc(f_scaled, 1)
                    dve.wait_ge(f_scaled, v + 1)
                    V.tensor_tensor(t3[:, :, :], f_sb[:, :, :], x2[:, :, :], ALU.add).then_inc(t3_ready, 1)
                    dve.wait_ge(t3_ready, v + 1)
                    layernorm_stats(2, t3, v)
                elif name == "ln3_apply":
                    dve.wait_ge(s_store, 16 * (v + 1))
                    layernorm_apply(2, out_sb, t3, v, out_ready)

            for b in (taken, e_sb, p_sb):
                last = V.memset(b[:], 0.0)
            last.then_inc(zeroed, 1)
            dve.wait_ge(zeroed, 1)
            walk("dve", step, dve)


_INPUTS = ["x", "xt", "ctx_w", "itok", "wqt", "bq", "wkt", "bk", "wvt", "bv", "wot", "bo", "w1t", "w2t", "ffnt",
           "c_ident", "c_hadamard", "c_causal", "c_heads"]


def kernel(x, ctx_512, itok_BxS2xS_0_7, L0_attn_Wq, L0_attn_bq, L0_attn_Wk, L0_attn_bk, L0_attn_Wv, L0_attn_bv,
           L0_attn_Wo, L0_attn_bo, L0_xattn_proj_in, L0_xattn_proj_out, L0_ffn_weight):
    import numpy as np
    import concourse.bacc as bacc
    from concourse import mybir as mb
    from concourse.bass_utils import run_bass_kernel_spmd

    had = np.array([[1.0]])
    while had.shape[0] < D:
        had = np.block([[had, had], [had, -had]])

    def by_chunk(bias):
        return np.asarray(bias).reshape(CD, P).T

    row, col = np.arange(P)[:, None], np.arange(P)[None, :]
    arrays = {
        "x": x, "xt": np.asarray(x).reshape(BATCH * SEQ, D).T, "ctx_w": np.asarray(ctx_512).transpose(0, 2, 1),
        "itok": np.asarray(itok_BxS2xS_0_7).transpose(0, 2, 1),
        "wqt": np.asarray(L0_attn_Wq).T, "bq": by_chunk(L0_attn_bq), "wkt": np.asarray(L0_attn_Wk).T, "bk": by_chunk(L0_attn_bk),
        "wvt": np.asarray(L0_attn_Wv).T, "bv": by_chunk(L0_attn_bv), "wot": np.asarray(L0_attn_Wo).T, "bo": L0_attn_bo,
        "w1t": np.asarray(L0_xattn_proj_in).transpose(0, 2, 1),
        "w2t": np.asarray(L0_xattn_proj_out).transpose(0, 2, 1),
        "ffnt": np.asarray(L0_ffn_weight).T,
        "c_ident": np.eye(P, dtype=np.float32),
        "c_hadamard": (had / np.sqrt(D)).astype(np.float32),
        "c_causal": np.concatenate([np.where(np.arange(QB * (j + 1)) > QB * j + row % QB, MASKED, 0.0)
                                    for j in range(BLOCKS)], axis=1).astype(np.float32),
        "c_heads": (row // DH == col[:, :HG]).astype(np.float32),
    }
    arrays = {f"in_{n}": np.ascontiguousarray(arrays[n]) for n in _INPUTS}
    nc = bacc.Bacc("TRN2", target_bir_lowering=False, num_devices=1)
    args = [nc.dram_tensor(n, a.shape, mb.dt.from_np(a.dtype), kind="ExternalInput").ap() for n, a in arrays.items()]
    out = nc.dram_tensor("out", (BATCH, SEQ, D), mb.dt.float32, kind="ExternalOutput").ap()
    decoder_layer(nc, *args, out)
    r = run_bass_kernel_spmd(nc, [arrays], core_ids=[0])
    return r.results[0]["out"]
```

```python
from contextlib import ExitStack

import concourse.bass as bass
from concourse import mybir

ALU = mybir.AluOpType
ACT = mybir.ActivationFunctionType
AX_X = mybir.AxisListType.X
F32 = mybir.dt.float32
BF16 = mybir.dt.bfloat16
F16 = mybir.dt.float16
I32 = mybir.dt.int32

P = 128
BATCH, SEQ, D = 16, 128, 256
HEADS = 16
DH = D // HEADS
TOPK = 32
EXPERTS, HIDDEN = 8, 512
CD = D // P
CH = HIDDEN // P
UB = 2
UT = UB * SEQ
UNITS = BATCH // UB
HG = P // DH
GROUPS = HEADS // HG
TILES = UB * GROUPS
QB = P // HG
BLOCKS = SEQ // QB
FREE_BLOCKS = TOPK // QB
HALF = BLOCKS // 2
VW = DH + 1
SCALE = DH ** -0.5
EPS = 1e-5
MASKED = -1e30
TAKEN = -3e38
ROUND = 1.5 * 2.0 ** 23
QPOS, QNEG = 7, 8
RING_STEPS = 2 * EXPERTS
STAGED = 2
EXPONENT = 1 << 23


def pitch(half):
    return QB * HALF * (half + 1)


def score_at(j):
    half = j // HALF
    return pitch(0) * HALF * half + pitch(half) * (HALF * (half + 1) - 1 - j)


def prob_at(j):
    return 64 * j if j < HALF else 64 * HALF + P * (j - HALF)


S_COLS = HALF * (pitch(0) + pitch(1))
P_COLS = prob_at(BLOCKS)
SEL_FROM = prob_at(FREE_BLOCKS)
ROUNDS = TOPK // 8
STAGES = 2 * ROUNDS - 1
SEL_GROUP = (BLOCKS - FREE_BLOCKS) // 2
SEL_STEPS = 2 * STAGES


def expert_steps():
    steps = [("L1", 0, 0), ("L1", 0, 1)]
    for e in range(1, EXPERTS):
        steps += [("L1", e, 0), ("L2", e - 1, 0), ("L1", e, 1), ("L2", e - 1, 1)]
    return steps + [("L2", EXPERTS - 1, 0), ("L2", EXPERTS - 1, 1)]


SLOTS = 4 * EXPERTS
STEADY = {
    "shift0": 0, "shift1": 0, "shift2": 0.5, "shift3": 0,
    "lag": 12, "gated_sum": 2,
    "exp": 2.5, "select": 1, "pace": 1, "keep": 5, "turn_probs": 7, "turn_probs2": 9, "attend": 10,
    "normalise": 10.5,
    "scores": 1, "scores_next_unit": 3, "copy_scores": 0,
    "v": 3.5, "q": 19.5, "k": 23.5, "spread_q": 19.5,
    "x_plus_bo": 1.5, "gate_sums": 3.5, "turn_o": 5, "out_proj": 7.5, "ln1_stats": 7, "ln1_apply": 8.5,
    "turn_x1": 9.5, "gate_scale": 13,
    "ln2_stats": 13.5, "ln2_apply": 16, "turn_x2": 16, "hadamard": 17, "quantise": 16.5, "to_q4": 17,
    "turn_q4": 21.5, "ffn": 22.5, "ln3_stats": 22, "ln3_apply": 25,
}
STARTING = STEADY | {
    "exp": 3, "keep": 6.5, "attend": 11.5, "scores": 0, "scores_next_unit": 1.5, "copy_scores": 1, "v": 5.5,
    "q": 22, "k": 23, "spread_q": 22,
}
FILLING = STEADY | {
    "shift1": 1, "shift2": 0, "pace": 1.25, "scores": 0, "scores_next_unit": 1.5, "copy_scores": 1, "v": 4,
    "q": 22.5, "k": 23, "spread_q": 23.5, "x_plus_bo": 0.5, "turn_o": 3, "out_proj": 4.5, "ln1_stats": 6,
    "ln1_apply": 7, "turn_x1": 8.5, "gate_scale": 18,
}
DRAINING = STEADY | {
    "turn_probs2": 7, "normalise": 11, "x_plus_bo": 3, "out_proj": 6, "ln1_apply": 7, "turn_x1": 8,
    "ln2_apply": 15, "turn_x2": 15.5, "hadamard": 18.5, "quantise": 17, "to_q4": 18.5, "ln3_apply": 27,
}
PREP_SLOTS = 5.5
PREP = {
    "load_w": 1.5, "w_squares": 0, "w_sum": 1, "w_scale": 1.5, "w_high": 2, "w1_low": 2.5, "w2_low": 4,
    "ffn_abs": 29.5, "ffn_sum": 32.5, "ffn_ternary": 34,
}


def build_schedule(iteration):
    slot = (STEADY if iteration is None else STARTING if iteration < 1 else FILLING if iteration < FIRST_LOOP
            else DRAINING)
    steps = expert_steps()
    placed = []

    def put(s, engine, name, off, *args):
        placed.append((s, (engine, name, off, args)))

    lag = slot["lag"]
    for s in range(SLOTS):
        kind, e, i = steps[(s - lag) % SLOTS]
        off = 1 if s >= lag else 2
        put(s, "pe", kind, off, e, i)
        if kind == "L1":
            put(s, "act", "relu", off, e, i)
            put(s, "pool", "h_low", off, e, i)
        s_sum = lag + slot["gated_sum"]
        kind, e, i = steps[(s - s_sum) % SLOTS]
        if kind == "L2" and i == 1:
            for b in range(UB):
                put(s, "dve", "gated_sum", 1 if s >= s_sum else 2, e, b)
    for k in range(TILES):
        b = (SLOTS // TILES) * k + slot[f"shift{k}"]
        put(b, "dve", "first_max", 0, k)
        put(b + slot["exp"], "act", "exp", 0, k)
        for r in range(STAGES):
            put(b + slot["select"] + r // 2 * slot["pace"], "dve", "select", 0, k, r)
        put(b + slot["keep"], "dve", "keep", 0, k)
        if k < TILES - 1:
            s, off, n = b + slot["scores"], 0, k + 1
        else:
            s, off, n = b + slot["scores_next_unit"], -1, 0
        put(s, "pe", "scores", off, n)
        put(s + slot["copy_scores"], "act", "copy_scores", off, n)
        for name in ("turn_probs", "turn_probs2", "attend", "normalise"):
            s, off = (b + slot[name], 0) if k < TILES - 1 else (max(b + slot[name] - SLOTS, 0), 1)
            if name in ("attend", "normalise"):
                put(s, "pe" if name == "attend" else "dve", name, off, k)
            else:
                half = int(name == "turn_probs2")
                put(s, "pe", "turn_probs", off, k, half)
                put(s, "act", "copy_probs", off, k, half)
    put(0, "sp", "load_ctx", 1)
    put(0, "sp", "load_x", 1)
    put(slot["v"], "pe", "v", 0)
    put(slot["v"], "act", "copy_v", 0)
    put(slot["v"] + 1, "sp", "load_xt", -1)
    put(slot["x_plus_bo"], "pool", "x_plus_bo", 1)
    for b in range(UB):
        put(slot["gate_sums"] + b, "dve", "gate_sums", 1, b)
    put(slot["turn_o"], "pe", "turn_o", 1)
    put(slot["turn_o"], "act", "copy_ot", 1)
    put(slot["out_proj"], "pe", "out_proj", 1)
    put(slot["ln1_stats"], "dve", "ln1_stats", 1)
    put(slot["ln1_stats"], "pool", "rstd", 1, 0)
    put(slot["ln1_apply"], "dve", "ln1_apply", 1)
    put(slot["turn_x1"], "pe", "turn_x1", 1)
    put(slot["turn_x1"], "act", "x1t_high", 1)
    put(slot["turn_x1"], "dve", "x1t_low", 1)
    put(slot["gate_scale"], "dve", "gate_scale", 1)
    put(slot["ln2_stats"], "dve", "ln2_stats", 2)
    put(slot["ln2_stats"], "pool", "rstd", 2, 1)
    put(slot["ln2_apply"], "dve", "ln2_apply", 2)
    put(slot["turn_x2"], "pe", "turn_x2", 2)
    put(slot["turn_x2"], "act", "x2t_high", 2)
    put(slot["turn_x2"], "dve", "x2t_low", 2)
    put(slot["hadamard"], "pe", "hadamard", 2)
    put(slot["quantise"], "dve", "quantise", 2)
    put(slot["to_q4"], "act", "to_q4", 2)
    put(slot["turn_q4"], "pe", "turn_q4", 2)
    put(slot["turn_q4"], "act", "copy_q4t", 2)
    put(slot["ffn"], "pe", "ffn", 2)
    put(slot["ln3_stats"], "dve", "ln3_stats", 2)
    put(slot["ln3_stats"], "pool", "rstd", 2, 2)
    put(slot["ln3_apply"], "dve", "ln3_apply", 2)
    put(slot["ln3_apply"], "sp", "store", 2)
    put(slot["q"], "pe", "q", -1)
    put(slot["q"], "act", "copy_q", -1)
    put(slot["k"], "pe", "k", -1)
    put(slot["k"], "act", "copy_k", -1)
    for k in range(TILES):
        put(slot["spread_q"] + k, "pool", "spread_q", -1, k)
    for e in range(EXPERTS):
        for engine, name in (("sp", "load_w"), ("act", "w_squares"), ("pe", "w_sum"), ("dve", "w_scale"),
                             ("act", "w_high"), ("pool", "w1_low"), ("pool", "w2_low")):
            first = PREP_SLOTS * e
            if name == "load_w":
                first = max(0, first - PREP_SLOTS * STAGED + max(PREP["w1_low"], PREP["w2_low"]))
            it, s = divmod(first + PREP[name], SLOTS)
            if it == iteration:
                put(s, engine, name, it, e)
    for engine, name in (("act", "ffn_abs"), ("pe", "ffn_sum"), ("dve", "ffn_ternary")):
        it, s = divmod(PREP[name], SLOTS)
        if it == iteration:
            put(s, engine, name, it)
    return [step for _, step in sorted(placed, key=lambda x: x[0])]


FIRST_LOOP, LAST_LOOP = 2, UNITS - 2
ITERATIONS = UNITS + 2
SCHEDULE = build_schedule(None)
SCHEDULES = {u: build_schedule(u) for u in (-1, 0, 1, UNITS, UNITS + 1)}


def decoder_layer(nc, x, xt, ctx_w, itok, wqt, bq, wkt, bk, wvt, bv, wot, bo, w1t, w2t, ffnt,
                  c_ident, c_hadamard, c_causal, c_heads, out):
    with ExitStack() as stack:
        def sb(name, shape, dt=F32):
            return stack.enter_context(nc.sbuf_tensor(name, shape, dt))

        def sem(name):
            return stack.enter_context(nc.semaphore(name))

        def bank(name):
            return stack.enter_context(nc.psum_tensor(name, [P, 512], F32))

        wq_sb, wk_sb, wv_sb, wo_sb = (sb(n, [P, CD, D]) for n in ("wq_sb", "wk_sb", "wv_sb", "wo_sb"))
        bq_sb, bk_sb, bv_sb = (sb(n, [P, CD]) for n in ("bq_sb", "bk_sb", "bv_sb"))
        bo_sb = sb("bo_sb", [P, D])
        w1_hi, w1_lo = (sb(n, [P, EXPERTS, CD, HIDDEN], F16) for n in ("w1_hi", "w1_lo"))
        w2_hi, w2_lo = (sb(n, [P, EXPERTS, CH, D], F16) for n in ("w2_hi", "w2_lo"))
        w1_raw = sb("w1_raw", [P, STAGED, CD, HIDDEN])
        w2_raw = sb("w2_raw", [P, STAGED, CH, D])
        w_sq = sb("w_sq", [P, EXPERTS, 2])
        w_ms = sb("w_ms", [P, EXPERTS, 2])
        w_half = sb("w_half", [P, EXPERTS, 2], I32)
        w_pow = sb("w_pow", [P, EXPERTS, 2])
        w_inv = sb("w_inv", [P, EXPERTS, 2])
        w_undo = sb("w_undo", [P, EXPERTS])
        had_sb = sb("had_sb", [P, CD, D])
        had_h = sb("had_h", [P, CD, D], F16)
        ffn_sb = sb("ffn_sb", [P, CD, D])
        tern_sb = sb("tern_sb", [P, CD, D], BF16)
        wscale = sb("wscale", [P, D])
        ident = sb("ident", [P, P])
        ident_h = sb("ident_h", [P, P], BF16)
        causal = sb("causal", [P, HALF * QB])
        causal_h = sb("causal_h", [P, HALF * QB], BF16)
        head_mask = sb("head_mask", [P, HG])
        ones = sb("ones", [P, P])
        minus_half = sb("minus_half", [P, UB])
        xt_sb = sb("xt_sb", [P, CD, UT])
        qt_sb = sb("qt_sb", [P, GROUPS, UT])
        kt_sb = sb("kt_sb", [P, GROUPS, UT])
        q_spread = sb("q_spread", [P, TILES, BLOCKS, HG, QB])
        v_sb = sb("v_sb", [P, UB * HEADS, VW])
        s_sb = sb("s_sb", [P, 2, S_COLS])
        top8 = sb("top8", [P, 2, BLOCKS, 8])
        next8 = sb("next8", [P, BLOCKS, 8])
        neg_max = sb("neg_max", [P, 2, BLOCKS])
        taken = sb("taken", [P, P_COLS])
        e_sb = sb("e_sb", [P, 2, P_COLS])
        p_sb = sb("p_sb", [P, 2, P_COLS])
        pt_sb = sb("pt_sb", [P, 2, HG, BLOCKS, QB])
        rsum = sb("rsum", [P, HG])
        o_sb = sb("o_sb", [P, UB, D])
        ot_sb = sb("ot_sb", [P, CD, UT])
        x_sb = sb("x_sb", [P, UB, D])
        xb_sb = sb("xb_sb", [P, UB, D])
        t1 = sb("t1", [P, UB, D])
        t3 = sb("t3", [P, UB, D])
        stats = sb("stats", [P, 3, UB, 6])
        meanvar = sb("meanvar", [P, 3, UB, 2])
        var_eps = sb("var_eps", [P, 3, UB])
        rstd = sb("rstd", [P, 3, UB])
        x1 = sb("x1", [P, UB, D])
        x1t_hi, x1t_lo = sb("x1t_hi", [P, CD, UT], F16), sb("x1t_lo", [P, CD, UT], F16)
        x2 = sb("x2", [P, UB, D])
        x2t_hi, x2t_lo = sb("x2t_hi", [P, CD, UT], F16), sb("x2t_lo", [P, CD, UT], F16)
        out_sb = sb("out_sb", [P, UB, D])
        ctx_sb = sb("ctx_sb", [P, UB, SEQ])
        itok_sb = sb("itok_sb", [P, UB, SEQ], I32)
        gate_part = sb("gate_part", [P, UB, EXPERTS, SEQ], BF16)
        gate_raw = sb("gate_raw", [P, UB, EXPERTS])
        gate = sb("gate", [P, UB, EXPERTS])
        h_raw = sb("h_raw", [P, 2, 2, UT])
        h_hi, h_lo = sb("h_hi", [P, 2, CH, UT], F16), sb("h_lo", [P, 2, CH, UT], F16)
        acc = sb("acc", [P, UB, D])
        amax = sb("amax", [P, UB])
        xscale = sb("xscale", [P, UB])
        xscale_inv = sb("xscale_inv", [P, UB])
        rounded = sb("rounded", [P, UB, D])
        clipped = sb("clipped", [P, UB, D])
        q4 = sb("q4", [P, UB, D], BF16)
        q4t = sb("q4t", [P, CD, UT], BF16)
        f_sb = sb("f_sb", [P, UB, D])
        tmp_a, tmp_b = rounded, clipped

        ps_hi, ps_lo, ps_pt, ps_misc = bank("ps_hi"), bank("ps_lo"), bank("ps_pt"), bank("ps_misc")
        ps_z = [bank("ps_z0"), bank("ps_z1")]
        ps_o = [bank("ps_o0"), bank("ps_o1")]
        misc_h = ps_misc[:, :].bitcast(BF16)

        s_const, s_qk, s_vo, s_ffnw = sem("s_const"), sem("s_qk"), sem("s_vo"), sem("s_ffnw")
        w_loaded = [sem(f"w_loaded{i}") for i in range(STAGED)]
        w_squared, w_summed, w_step, w_high_ready, w1_low_step, w2_low_step, w2_low_ready, w_undo_step, had_cast = (
            sem(n) for n in ("w_squared", "w_summed", "w_step", "w_high_ready", "w1_low_step", "w2_low_step",
                             "w2_low_ready",
                             "w_undo_step", "had_cast"))
        s_xt, s_x, s_ctx, s_store = sem("xt_loaded"), sem("x_loaded"), sem("ctx_loaded"), sem("out_stored")
        zeroed, pool_const, cast_done, ffn_prep, ffn_abs, ffn_sum = (
            sem("zeroed"), sem("pool_const"), sem("cast_done"), sem("ffn_prep"), sem("ffn_abs"), sem("ffn_sum"))
        q_ready, k_ready, v_ready, s_ready, pt_ready, pv_ready = (
            sem(n) for n in ("q_ready", "k_ready", "v_ready", "s_ready", "pt_ready", "pv_ready"))
        ot_ready, y_ready, x1t_ready, l1_done, l2_done = (
            sem(n) for n in ("ot_ready", "y_ready", "x1t_ready", "l1_done", "l2_done"))
        x2t_ready, xh_ready, q4t_ready, f_ready = (
            sem(n) for n in ("x2t_ready", "xh_ready", "q4t_ready", "f_ready"))
        q_copied, k_copied, v_copied, s_copied, pt_copied, ot_copied = (
            sem(n) for n in ("q_copied", "k_copied", "v_copied", "s_copied", "pt_copied", "ot_copied"))
        x1t_high, x2t_high, q4t_copied, relu_done, e_ready, q4_ready = (
            sem(n) for n in ("x1t_high", "x2t_high", "q4t_copied", "relu_done", "e_ready", "q4_ready"))
        x1t_low, x2t_low, w1_low_ready = sem("x1t_low"), sem("x2t_low"), sem("w1_low_ready")
        max_ready, nmax_ready, sel_step, p_ready, rsum_ready, o_ready = (
            sem(n) for n in ("max_ready", "nmax_ready", "sel_step", "p_ready", "rsum_ready", "o_ready"))
        t1_ready, t3_ready, gate_summed, gate_ready, acc_done, x1_ready, x2_ready, out_ready = (
            sem(n) for n in ("t1_ready", "t3_ready", "gate_summed", "gate_ready", "acc_done", "x1_ready",
                             "x2_ready", "out_ready"))
        stat_step = [sem(f"stat_step{i}") for i in range(3)]
        dve_held, pool_held = sem("dve_held"), sem("pool_held")
        quant_step, inv_ready, f_scaled = sem("quant_step"), sem("inv_ready"), sem("f_scaled")
        spread_ready, xb_ready, h_low_done = sem("spread_ready"), sem("xb_ready"), sem("h_low_done")
        eps_added = [sem(f"eps_added{i}") for i in range(3)]
        rstd_ready = [sem(f"rstd_ready{i}") for i in range(3)]

        MISC = {
            "q": (q_copied, 1, lambda k: 1), "k": (k_copied, 1, lambda k: 1), "v": (v_copied, 1, lambda k: 1),
            "attend": (o_ready, TILES, lambda k: k + 1), "turn_o": (ot_copied, 1, lambda k: 1),
            "out_proj": (t1_ready, 1, lambda k: 1), "turn_x1": (x1t_low, 1, lambda k: 1),
            "turn_x2": (x2t_low, 1, lambda k: 1),
            "hadamard": (quant_step, 4, lambda k: 3), "turn_q4": (q4t_copied, 1, lambda k: 1),
            "ffn": (f_scaled, 1, lambda k: 1),
        }

        def walk(engine, step, eng):
            def iteration(u, inside):
                for e, name, off, args in (SCHEDULE if inside else SCHEDULES.get(u, SCHEDULE)):
                    if e == engine and (inside or 0 <= u - off < UNITS):
                        step(name, u - off, off, *args)
            for u in range(-1, FIRST_LOOP):
                iteration(u, False)
            with eng.Fori(FIRST_LOOP, LAST_LOOP + 1) as u:
                iteration(u, True)
            for u in range(LAST_LOOP + 1, ITERATIONS):
                iteration(u, False)

        def wait(eng, s, value):
            if not isinstance(value, int) or value > 0:
                eng.wait_ge(s, value)

        block = stack.enter_context(nc.Block())

        @block.sync
        def _(sp):
            def rows(a):
                return a.rearrange("(c p) n -> p c n", p=P)

            def load_xt(v):
                wait(sp, v_ready, v)
                sp.dma_start(xt_sb[:, :, :], rows(xt)[:, :, bass.ds(v * UT, UT)]).then_inc(s_xt, 16)

            def step(name, v, off, *args):
                if name == "load_xt":
                    if not isinstance(v, int) or v > 0:
                        load_xt(v)
                elif name == "load_x":
                    wait(sp, xb_ready, v)
                    sp.dma_start(x_sb[:, :, :], x.rearrange("b s d -> s b d")[:, bass.ds(v * UB, UB), :])\
                        .then_inc(s_x, 16)
                elif name == "load_ctx":
                    wait(sp, gate_summed, UB * v)
                    sp.dma_start(ctx_sb[:, :, :], ctx_w.rearrange("b s k -> s b k")[:, bass.ds(v * UB, UB), :])\
                        .then_inc(s_ctx, 16)
                    sp.dma_start(itok_sb[:, :, :], itok.rearrange("b s k -> s b k")[:, bass.ds(v * UB, UB), :])\
                        .then_inc(s_ctx, 16)
                elif name == "load_w":
                    e, = args
                    wait(sp, w1_low_ready, e - STAGED + 1)
                    wait(sp, w2_low_ready, e - STAGED + 1)
                    sp.dma_start(w1_raw[:, e % STAGED, :, :], rows(w1t[e])).then_inc(w_loaded[e % STAGED], 16)
                    sp.dma_start(w2_raw[:, e % STAGED, :, :], rows(w2t[e])).then_inc(w_loaded[e % STAGED], 16)
                elif name == "store":
                    sp.wait_ge(out_ready, v + 1)
                    sp.dma_start(out.rearrange("b s d -> s b d")[:, bass.ds(v * UB, UB), :], out_sb[:, :, :])\
                        .then_inc(s_store, 16)

            sp.dma_start(wq_sb[:, :, :], rows(wqt)).then_inc(s_qk, 16)
            load_xt(0)
            sp.dma_start(wk_sb[:, :, :], rows(wkt)).then_inc(s_qk, 16)
            for dst, src in ((bq_sb, bq), (bk_sb, bk), (head_mask, c_heads), (causal, c_causal), (ident, c_ident)):
                sp.dma_start(dst[:, :], src[:, :]).then_inc(s_const, 16)
            sp.dma_start(wv_sb[:, :, :], rows(wvt)).then_inc(s_vo, 16)
            sp.dma_start(ffn_sb[:, :, :], rows(ffnt)).then_inc(s_ffnw, 16)
            sp.dma_start(had_sb[:, :, :], rows(c_hadamard)).then_inc(s_ffnw, 16)
            sp.dma_start(wo_sb[:, :, :], rows(wot)).then_inc(s_vo, 16)
            sp.dma_start(bv_sb[:, :], bv[:, :]).then_inc(s_vo, 16)
            sp.dma_start(bo_sb[:, :], bo.rearrange("(a n) -> a n", a=1).broadcast_to([P, D])).then_inc(s_vo, 16)
            sp.sem_inc(s_store, 16)
            walk("sp", step, sp)
            sp.wait_ge(s_store, 16 * (UNITS + 1))

        CONSTS = 5 * 16

        @block.gpsimd
        def _(pool):
            nc.gpsimd.memset(minus_half[:, :], -0.5)
            nc.gpsimd.memset(ones[:, :], 1.0)
            nc.gpsimd.memset(v_sb[:, :, DH:VW], 1.0)
            nc.gpsimd.memset(pt_sb[:, :, :, :, :], 0.0).then_inc(pool_const, 1)
            pool.wait_ge(s_const, CONSTS)

            def step(name, v, off, *args):
                if name == "spread_q":
                    k, = args
                    b, g = divmod(k, GROUPS)
                    pool.wait_ge(q_copied, v + 1)
                    wait(pool, s_ready, 2 * (TILES * (v - 1) + k) + 2)
                    q_in = qt_sb[:, g, b * SEQ:(b + 1) * SEQ].rearrange("p (j a q) -> p j a q", a=1, q=QB)
                    nc.gpsimd.tensor_tensor(
                        q_spread[:, k, :, :, :], q_in.broadcast_to([P, BLOCKS, HG, QB]),
                        head_mask[:, :].rearrange("p (a h c) -> p a h c", a=1, c=1).broadcast_to([P, BLOCKS, HG, QB]),
                        ALU.mult).then_inc(spread_ready, 1)
                elif name == "x_plus_bo":
                    pool.wait_ge(s_x, 16 * (v + 1))
                    if isinstance(v, int) and v == 0:
                        pool.wait_ge(s_vo, 64)
                    wait(pool, t1_ready, v)
                    for b in range(UB):
                        last = nc.gpsimd.tensor_tensor(xb_sb[:, b, :], x_sb[:, b, :], bo_sb[:, :], ALU.add)
                    last.then_inc(xb_ready, 1)
                elif name == "h_low":
                    e, z = args
                    i = RING_STEPS * v + 2 * e + z
                    pool.wait_ge(relu_done, 2 * i + 2)
                    wait(pool, l2_done, RING_STEPS * v + 2 * e - 2)
                    nc.gpsimd.tensor_tensor(h_lo[:, e % 2, 2 * z:2 * z + 2, :], h_raw[:, z, :, :],
                                            h_hi[:, e % 2, 2 * z:2 * z + 2, :], ALU.subtract)\
                        .then_inc(h_low_done, 1)
                elif name in ("w1_low", "w2_low"):
                    e, = args
                    i, raw, hi, lo, step_done, ready = (
                        (0, w1_raw, w1_hi, w1_lo, w1_low_step, w1_low_ready) if name == "w1_low" else
                        (1, w2_raw, w2_hi, w2_lo, w2_low_step, w2_low_ready))
                    pool.wait_ge(w_high_ready, 2 * e + i + 1)
                    nc.gpsimd.tensor_scalar(raw[:, e % STAGED, :, :], raw[:, e % STAGED, :, :],
                                            w_pow[:, e, i:i + 1], 1.0, ALU.mult, ALU.mult).then_inc(step_done, 1)
                    pool.wait_ge(step_done, e + 1)
                    nc.gpsimd.tensor_tensor(lo[:, e, :, :], raw[:, e % STAGED, :, :], hi[:, e, :, :],
                                            ALU.subtract).then_inc(ready, 1)
                elif name == "rstd":
                    i, = args
                    pool.wait_ge(stat_step[i], 2 * (v + 1))
                    pool.sem_inc(pool_held, 1)
                    nc.gpsimd.tensor_scalar(var_eps[:, i, :], meanvar[:, i, :, 1], EPS, None, ALU.add)\
                        .then_inc(eps_added[i], 1)
                    pool.wait_ge(eps_added[i], v + 1)
                    nc.gpsimd.tensor_tensor(rstd[:, i, :], var_eps[:, i, :], minus_half[:, :], ALU.pow)\
                        .then_inc(rstd_ready[i], 1)

            walk("pool", step, pool)

        @block.scalar
        def _(act):
            act.wait_ge(s_const, CONSTS)
            act.activation(ident_h[:, :], ident[:, :], ACT.Copy)
            act.activation(causal_h[:, :], causal[:, :], ACT.Copy).then_inc(cast_done, 1)

            def step(name, v, off, *args):
                n = TILES * v + args[0] if name in ("exp", "copy_scores", "copy_probs") else None
                if name == "copy_q" or name == "copy_k":
                    ready, dst, bias, copied = ((q_ready, qt_sb, bq_sb, q_copied) if name == "copy_q"
                                                else (k_ready, kt_sb, bk_sb, k_copied))
                    act.wait_ge(ready, v + 1)
                    if name == "copy_q":
                        wait(act, spread_ready, TILES * v)
                    for g in range(GROUPS):
                        last = act.activation(dst[:, g, :], ps_misc[:, g * UT:(g + 1) * UT], ACT.Identity,
                                              bias=bias[:, g:g + 1])
                    last.then_inc(copied, 1)
                elif name == "copy_v":
                    act.wait_ge(v_ready, v + 1)
                    act.activation(v_sb[:, :, 0:DH], ps_misc[:, :].rearrange("p (h d) -> p h d", d=DH), ACT.Copy)\
                        .then_inc(v_copied, 1)
                elif name == "copy_scores":
                    k, = args
                    wait(act, p_ready, n - 1)
                    act.wait_ge(s_ready, 2 * n + 1)
                    act.activation(s_sb[:, k % 2, HALF * pitch(0):S_COLS], ps_hi[:, 0:HALF * pitch(1)],
                                   ACT.Copy).then_inc(s_copied, 1)
                    act.wait_ge(s_ready, 2 * n + 2)
                    act.activation(s_sb[:, k % 2, 0:HALF * pitch(0)], ps_lo[:, 0:HALF * pitch(0)],
                                   ACT.Copy).then_inc(s_copied, 1)
                elif name == "exp":
                    k, = args
                    act.wait_ge(nmax_ready, n + 1)
                    wait(act, p_ready, n - 1)
                    wait(act, pt_ready, 2 * n - 2)
                    for j in range(BLOCKS):
                        m = QB * (j + 1)
                        dst = p_sb if j < FREE_BLOCKS else e_sb
                        last = act.activation(dst[:, k % 2, prob_at(j):prob_at(j) + m],
                                              s_sb[:, k % 2, score_at(j):score_at(j) + m], ACT.Exp,
                                              bias=neg_max[:, k % 2, j:j + 1], scale=SCALE)
                    last.then_inc(e_ready, 1)
                elif name == "copy_probs":
                    k, half = args
                    rows = P if half else P // 2
                    act.wait_ge(pt_ready, 2 * n + half + 1)
                    wait(act, pv_ready, n - 1)
                    act.activation(
                        pt_sb[0:rows, k % 2, :, HALF * half:HALF * (half + 1), :].rearrange("p h j q -> p j h q"),
                        ps_pt[0:rows, :].rearrange("p (j h q) -> p j h q", h=HG, q=QB), ACT.Copy)\
                        .then_inc(pt_copied, 1)
                elif name == "copy_ot":
                    act.wait_ge(ot_ready, v + 1)
                    if isinstance(v, int) and v == 0:
                        act.wait_ge(s_vo, 64)
                    for c in range(CD):
                        last = act.activation(ot_sb[:, c, :], ps_misc[:, c * UT:(c + 1) * UT], ACT.Identity,
                                              bias=bv_sb[:, c:c + 1])
                    last.then_inc(ot_copied, 1)
                elif name in ("x1t_high", "x2t_high"):
                    ready, dst, done = ((x1t_ready, x1t_hi, x1t_high) if name == "x1t_high"
                                        else (x2t_ready, x2t_hi, x2t_high))
                    act.wait_ge(ready, v + 1)
                    act.activation(dst[:, :, :], ps_misc[:, :].rearrange("p (c t) -> p c t", c=CD), ACT.Copy)\
                        .then_inc(done, 1)
                elif name == "relu":
                    e, z = args
                    i = RING_STEPS * v + 2 * e + z
                    act.wait_ge(l1_done, i + 1)
                    wait(act, l2_done, RING_STEPS * v + 2 * e - 2)
                    act.activation(h_hi[:, e % 2, 2 * z:2 * z + 2, :],
                                   ps_z[z][:, :].rearrange("p (c t) -> p c t", c=2), ACT.Relu)\
                        .then_inc(relu_done, 1)
                    wait(act, h_low_done, i - 1)
                    act.activation(h_raw[:, z, :, :],
                                   ps_z[z][:, :].rearrange("p (c t) -> p c t", c=2), ACT.Relu)\
                        .then_inc(relu_done, 1)
                elif name == "ffn_abs":
                    act.wait_ge(s_ffnw, 32)
                    act.activation(tmp_a[:, :, :], ffn_sb[:, :, :], ACT.Abs).then_inc(ffn_abs, 1)
                    act.activation(had_h[:, :, :], had_sb[:, :, :], ACT.Copy).then_inc(had_cast, 1)
                elif name == "w_squares":
                    e, = args
                    act.wait_ge(w_loaded[e % STAGED], 32 * (e // STAGED + 1))
                    act.activation(w1_hi[:, e, :, :], w1_raw[:, e % STAGED, :, :], ACT.Square,
                                   accum_out=w_sq[:, e, 0:1])
                    act.activation(w2_hi[:, e, :, :], w2_raw[:, e % STAGED, :, :], ACT.Square,
                                   accum_out=w_sq[:, e, 1:2]).then_inc(w_squared, 1)
                elif name == "w_high":
                    e, = args
                    act.wait_ge(w_step, 3 * (e + 1))
                    act.activation(w1_hi[:, e, :, :], w1_raw[:, e % STAGED, :, :], ACT.Copy,
                                   scale=w_pow[:, e, 0:1]).then_inc(w_high_ready, 1)
                    act.activation(w2_hi[:, e, :, :], w2_raw[:, e % STAGED, :, :], ACT.Copy,
                                   scale=w_pow[:, e, 1:2]).then_inc(w_high_ready, 1)
                elif name == "to_q4":
                    act.wait_ge(quant_step, 4 * (v + 1))
                    act.activation(q4[:, :, :], clipped[:, :, :], ACT.Copy, bias=-ROUND).then_inc(q4_ready, 1)
                elif name == "copy_q4t":
                    act.wait_ge(q4t_ready, v + 1)
                    act.activation(q4t[:, :, :], misc_h[:, 0:CD * UT].rearrange("p (c t) -> p c t", c=CD), ACT.Copy)\
                        .then_inc(q4t_copied, 1)

            walk("act", step, act)

        @block.tensor
        def _(pe):
            misc_before = [None]

            def take_misc(name, v, off, k=0):
                if misc_before[0] is not None:
                    s, per_unit, count, v0, off0, k0 = misc_before[0]
                    if not isinstance(v, int) and isinstance(v0, int):
                        v0 = v + (off - off0 - 1)
                    elif isinstance(v, int) and not isinstance(v0, int):
                        v0 = LAST_LOOP - off0
                    pe.wait_ge(s, v0 * per_unit + count(k0))
                misc_before[0] = (*MISC[name], v, off, k)

            def project(w, ready):
                for g in range(GROUPS):
                    for c in range(CD):
                        last = pe.matmul(ps_misc[:, g * UT:(g + 1) * UT], w[:, c, g * P:(g + 1) * P],
                                         xt_sb[:, c, :], start=c == 0, stop=c == CD - 1)
                last.then_inc(ready, 1)

            def rows_by(lhs_parts, rhs, ready):
                terms = [(lhs, c) for c in range(CD) for lhs in lhs_parts]
                for b in range(UB):
                    for n, (lhs, c) in enumerate(terms):
                        last = pe.matmul(ps_misc[:, b * D:(b + 1) * D], lhs[:, c, b * SEQ:(b + 1) * SEQ],
                                         rhs[:, c, :], start=n == 0, stop=n == len(terms) - 1)
                last.then_inc(ready, 1)

            def turn(src, idn, ready, dst):
                for c in range(CD):
                    for b in range(UB):
                        last = pe.transpose(dst[:, c * UT + b * SEQ:c * UT + (b + 1) * SEQ],
                                            src[:, b, c * P:(c + 1) * P], idn[:, :])
                last.then_inc(ready, 1)

            def step(name, v, off, *args):
                if name in MISC:
                    take_misc(name, v, off, *args)
                if name == "q":
                    pe.wait_ge(s_xt, 16 * (v + 1))
                    project(wq_sb, q_ready)
                elif name == "k":
                    project(wk_sb, k_ready)
                elif name == "v":
                    if off == 0 and isinstance(v, int) and v == 0:
                        pe.wait_ge(s_vo, 64)
                    rows_by([xt_sb], wv_sb, v_ready)
                elif name == "ffn_sum":
                    pe.wait_ge(pool_const, 1)
                    pe.wait_ge(ffn_abs, 1)
                    for c in range(CD):
                        last = pe.matmul(ps_o[1][:, 0:D], ones[:, :], tmp_a[:, c, :], start=c == 0, stop=c == CD - 1)
                    last.then_inc(ffn_sum, 1)
                elif name == "scores":
                    k, = args
                    n = TILES * v + k
                    b, g = divmod(k, GROUPS)
                    if k == 0 and isinstance(v, int) and v == 0:
                        pe.wait_ge(cast_done, 1)
                    pe.wait_ge(spread_ready, n + 1)
                    pe.wait_ge(k_copied, v + 1)
                    for half, ps in ((1, ps_hi), (0, ps_lo)):
                        wait(pe, s_copied, 2 * n - half)
                        m = pitch(half)
                        for i in range(HALF):
                            j = HALF * (half + 1) - 1 - i
                            pe.matmul(ps[:, m * i:m * (i + 1)], q_spread[:, k, j, :, :].rearrange("p h q -> p (h q)"),
                                      kt_sb[:, g, b * SEQ:b * SEQ + m], start=i == 0, stop=True,
                                      skip_group_check=True)
                        own = ps[:, QB:QB + HALF * (m - QB)].rearrange("p (i c) -> p i c", i=HALF)
                        own = own[:, :, m - 2 * QB:m - QB]
                        last = pe.matmul(own, ident_h[:, :], causal_h[:, :].rearrange("p (i c) -> p i c", i=HALF),
                                         start=False, stop=True, skip_group_check=True)
                        last.then_inc(s_ready, 1)
                elif name == "turn_probs":
                    k, half = args
                    n = TILES * v + k
                    pe.wait_ge(p_ready, n + 1)
                    wait(pe, pt_copied, 2 * n + half)
                    for i in range(HALF):
                        at = prob_at(HALF * half + i)
                        last = pe.transpose(ps_pt[:, i * P:(i + 1) * P], p_sb[:, k % 2, at:at + P], ident[:, :])
                    last.then_inc(pt_ready, 1)
                elif name == "attend":
                    k, = args
                    n = TILES * v + k
                    b, g = divmod(k, GROUPS)
                    pe.wait_ge(pt_copied, 2 * n + 2)
                    pe.wait_ge(v_copied, v + 1)
                    for h in range(HG):
                        last = pe.matmul(ps_misc[:, h * VW:(h + 1) * VW],
                                         pt_sb[:, k % 2, h, :, :].rearrange("p j q -> p (j q)"),
                                         v_sb[:, b * HEADS + g * HG + h, :], start=True, stop=True)
                    last.then_inc(pv_ready, 1)
                elif name == "turn_o":
                    pe.wait_ge(o_ready, TILES * (v + 1))
                    turn(o_sb, ident, ot_ready, ps_misc)
                elif name == "out_proj":
                    pe.wait_ge(ot_copied, v + 1)
                    rows_by([ot_sb], wo_sb, y_ready)
                elif name == "turn_x1":
                    pe.wait_ge(x1_ready, v + 1)
                    turn(x1, ident, x1t_ready, ps_misc)
                elif name == "L1":
                    e, z = args
                    i = RING_STEPS * v + 2 * e + z
                    if e == 0 and z == 0:
                        pe.wait_ge(x1t_low, v + 1)
                    if off == 2 or isinstance(v, int):
                        pe.wait_ge(w1_low_ready, e + 1)
                    wait(pe, relu_done, 2 * i - 2)
                    for d in range(2):
                        at = (2 * z + d) * P
                        terms = [(w, x, c) for c in range(CD) for w, x in ((w1_lo, x1t_hi), (w1_hi, x1t_lo),
                                                                           (w1_hi, x1t_hi))]
                        for n, (w, x, c) in enumerate(terms):
                            last = pe.matmul(ps_z[z][:, d * UT:(d + 1) * UT], w[:, e, c, at:at + P], x[:, c, :],
                                             start=n == 0, stop=n == len(terms) - 1)
                    last.then_inc(l1_done, 1)
                elif name == "L2":
                    e, b = args
                    i = RING_STEPS * v + 2 * e + b
                    if off == 2 or isinstance(v, int):
                        pe.wait_ge(w2_low_ready, e + 1)
                    pe.wait_ge(h_low_done, RING_STEPS * v + 2 * e + 2)
                    wait(pe, acc_done, i - b - 2)
                    if isinstance(v, int) and v == 0 and e == 0:
                        pe.wait_ge(w_step, 3 * EXPERTS - 2)
                        pe.wait_ge(ffn_prep, 1)
                    terms = [(h, w, c) for c in range(CH) for h, w in ((h_lo, w2_hi), (h_hi, w2_lo), (h_hi, w2_hi))]
                    for n, (h, w, c) in enumerate(terms):
                        last = pe.matmul(ps_o[e % 2][:, b * D:(b + 1) * D],
                                         h[:, e % 2, c, b * SEQ:(b + 1) * SEQ], w[:, e, c, :],
                                         start=n == 0, stop=n == len(terms) - 1)
                    last.then_inc(l2_done, 1)
                elif name == "w_sum":
                    e, = args
                    pe.wait_ge(w_squared, e + 1)
                    wait(pe, w_step, 3 * e - 2)
                    pe.matmul(ps_o[0][:, 0:2], ones[:, :], w_sq[:, e, :], start=True, stop=True)\
                        .then_inc(w_summed, 1)
                elif name == "turn_x2":
                    pe.wait_ge(x2_ready, v + 1)
                    turn(x2, ident, x2t_ready, ps_misc)
                elif name == "hadamard":
                    pe.wait_ge(x2t_low, v + 1)
                    pe.wait_ge(had_cast, 1)
                    rows_by([x2t_lo, x2t_hi], had_h, xh_ready)
                elif name == "turn_q4":
                    pe.wait_ge(q4_ready, v + 1)
                    turn(q4, ident_h, q4t_ready, misc_h)
                elif name == "ffn":
                    pe.wait_ge(q4t_copied, v + 1)
                    pe.wait_ge(ffn_prep, 3)
                    rows_by([q4t], tern_sb, f_ready)

            pe.wait_ge(s_qk, 32)
            walk("pe", step, pe)

        @block.vector
        def _(dve):
            V = nc.vector

            def layernorm_stats(i, src, v):
                for b in range(UB):
                    last = V.bn_stats(stats[:, i, b, :], src[:, b, :])
                last.then_inc(stat_step[i], 1)
                dve.wait_ge(stat_step[i], 2 * v + 1)
                dve.sem_inc(dve_held, 1)
                for b in range(UB):
                    last = V.bn_aggr(meanvar[:, i, b, :], stats[:, i, b, :])
                last.then_inc(stat_step[i], 1)

            def layernorm_apply(i, dst, src, v, ready):
                dve.wait_ge(rstd_ready[i], v + 1)
                for b in range(UB):
                    last = V.tensor_scalar(dst[:, b, :], src[:, b, :], meanvar[:, i, b, 0:1], rstd[:, i, b:b + 1],
                                           ALU.subtract, ALU.mult)
                last.then_inc(ready, 1)

            def step(name, v, off, *args):
                if name == "first_max":
                    k, = args
                    n = TILES * v + k
                    dve.wait_ge(s_copied, 2 * n + 2)
                    wait(dve, e_ready, n - 1)
                    dve.sem_inc(dve_held, 1)
                    for j in range(BLOCKS):
                        last = V.max(top8[:, k % 2, j, :],
                                     s_sb[:, k % 2, score_at(j):score_at(j) + QB * (j + 1)])
                    last.then_inc(max_ready, 1)
                    dve.wait_ge(max_ready, n + 1)
                    V.tensor_scalar(neg_max[:, k % 2, :], top8[:, k % 2, :, 0], -SCALE, None, ALU.mult)\
                        .then_inc(nmax_ready, 1)
                elif name == "select":
                    k, r = args
                    n = TILES * v + k
                    if r == 0:
                        wait(dve, p_ready, n)
                    for i, j in enumerate(range(FREE_BLOCKS, BLOCKS)):
                        m = QB * (j + 1)
                        t = taken[:, prob_at(j):prob_at(j) + m]
                        if r > 0 and i % SEL_GROUP == 0:
                            dve.wait_ge(sel_step, SEL_STEPS * n + 2 * (r - 1) + i // SEL_GROUP + 1)
                        if i % SEL_GROUP == 0:
                            dve.sem_inc(dve_held, 1)
                        if r % 2 == 1:
                            last = V.max(next8[:, j, :], t)
                        elif r == 0:
                            last = V.match_replace(t, top8[:, k % 2, j, :],
                                                   s_sb[:, k % 2, score_at(j):score_at(j) + m], TAKEN)
                        else:
                            last = V.match_replace(t, next8[:, j, :], t, TAKEN)
                        if i % SEL_GROUP == SEL_GROUP - 1:
                            last.then_inc(sel_step, 1)
                elif name == "keep":
                    k, = args
                    n = TILES * v + k
                    dve.wait_ge(e_ready, n + 1)
                    dve.wait_ge(sel_step, SEL_STEPS * (n + 1))
                    wait(dve, pt_ready, 2 * n - 2)
                    V.scalar_tensor_tensor(p_sb[:, k % 2, SEL_FROM:P_COLS], taken[:, SEL_FROM:P_COLS], TAKEN,
                                           e_sb[:, k % 2, SEL_FROM:P_COLS], ALU.is_equal, ALU.mult)\
                        .then_inc(p_ready, 1)
                elif name == "normalise":
                    k, = args
                    n = TILES * v + k
                    b, g = divmod(k, GROUPS)
                    dve.wait_ge(pv_ready, n + 1)
                    wait(dve, ot_ready, v)
                    pv = ps_misc[:, 0:HG * VW].rearrange("p (h c) -> p h c", c=VW)
                    V.reciprocal(rsum[:, :], pv[:, :, DH]).then_inc(rsum_ready, 1)
                    dve.wait_ge(rsum_ready, n + 1)
                    V.tensor_tensor(o_sb[:, b, g * P:(g + 1) * P].rearrange("p (h c) -> p h c", c=DH),
                                    pv[:, :, 0:DH],
                                    rsum[:, :].rearrange("p (h a) -> p h a", a=1).broadcast_to([P, HG, DH]),
                                    ALU.mult).then_inc(o_ready, 1)
                elif name == "ln1_stats":
                    dve.wait_ge(y_ready, v + 1)
                    dve.wait_ge(xb_ready, v + 1)
                    V.tensor_tensor(t1[:, :, :], ps_misc[:, :].rearrange("p (b n) -> p b n", b=UB),
                                    xb_sb[:, :, :], ALU.add).then_inc(t1_ready, 1)
                    dve.wait_ge(t1_ready, v + 1)
                    layernorm_stats(0, t1, v)
                elif name == "ln1_apply":
                    layernorm_apply(0, x1, t1, v, x1_ready)
                elif name == "gate_sums":
                    b, = args
                    dve.wait_ge(s_ctx, 32 * (v + 1))
                    for e in range(EXPERTS):
                        last = V.scalar_tensor_tensor(gate_part[:, b, e, :], itok_sb[:, b, :], float(e),
                                                      ctx_sb[:, b, :], ALU.is_equal, ALU.mult,
                                                      accum_out=gate_raw[:, b, e:e + 1])
                    last.then_inc(gate_summed, 1)
                elif name == "gate_scale":
                    dve.wait_ge(gate_summed, UB * (v + 1))
                    dve.wait_ge(w_undo_step, 2)
                    wait(dve, acc_done, RING_STEPS * v)
                    undo = w_undo[:, :].rearrange("p (b e) -> p b e", b=1).broadcast_to([P, UB, EXPERTS])
                    V.tensor_tensor(gate[:, :, :], gate_raw[:, :, :], undo, ALU.mult).then_inc(gate_ready, 1)
                elif name in ("x1t_low", "x2t_low"):
                    high, hi, lo, done = ((x1t_high, x1t_hi, x1t_lo, x1t_low) if name == "x1t_low"
                                          else (x2t_high, x2t_hi, x2t_lo, x2t_low))
                    dve.wait_ge(high, v + 1)
                    V.tensor_tensor(lo[:, :, :], ps_misc[:, :].rearrange("p (c t) -> p c t", c=CD), hi[:, :, :],
                                    ALU.subtract).then_inc(done, 1)
                elif name == "ffn_ternary":
                    dve.wait_ge(ffn_sum, 1)
                    V.tensor_scalar(wscale[:, :], ps_o[1][:, 0:D], 1.0 / D, 1e-5, ALU.mult, ALU.max)\
                        .then_inc(ffn_prep, 1)
                    dve.wait_ge(ffn_prep, 1)
                    for c in range(CD):
                        V.scalar_tensor_tensor(tmp_a[:, c, :], wscale[:, :], 0.5, ffn_sb[:, c, :], ALU.mult,
                                               ALU.is_lt)
                        last = V.scalar_tensor_tensor(tmp_b[:, c, :], wscale[:, :], -0.5, ffn_sb[:, c, :], ALU.mult,
                                                      ALU.is_gt)
                    last.then_inc(ffn_prep, 1)
                    dve.wait_ge(ffn_prep, 2)
                    V.tensor_tensor(tern_sb[:, :, :], tmp_a[:, :, :], tmp_b[:, :, :], ALU.subtract)\
                        .then_inc(ffn_prep, 1)
                elif name == "w_scale":
                    e, = args
                    dve.wait_ge(w_summed, e + 1)
                    V.tensor_scalar(w_ms[:, e, :], ps_o[0][:, 0:2], 1.0 / (HIDDEN * D), 1e-36, ALU.mult, ALU.max)\
                        .then_inc(w_step, 1)
                    dve.wait_ge(w_step, 3 * e + 1)
                    V.tensor_scalar(w_half[:, e, :], w_ms[:, e, :].bitcast(I32), 24, None, ALU.logical_shift_right)\
                        .then_inc(w_step, 1)
                    dve.wait_ge(w_step, 3 * e + 2)
                    V.tensor_scalar(w_pow[:, e, :].bitcast(I32), w_half[:, e, :], -float(EXPONENT),
                                    190.0 * EXPONENT, ALU.mult, ALU.add).then_inc(w_step, 1)
                    if e == EXPERTS - 1:
                        dve.wait_ge(w_step, 3 * EXPERTS)
                        V.tensor_scalar(w_inv[:, :, :].bitcast(I32), w_pow[:, :, :].bitcast(I32), -1.0,
                                        254.0 * EXPONENT, ALU.mult, ALU.add).then_inc(w_undo_step, 1)
                        dve.wait_ge(w_undo_step, 1)
                        V.tensor_tensor(w_undo[:, :], w_inv[:, :, 0], w_inv[:, :, 1], ALU.mult)\
                            .then_inc(w_undo_step, 1)
                elif name == "gated_sum":
                    e, b = args
                    i = RING_STEPS * v + 2 * e + b
                    dve.wait_ge(l2_done, i - b + 2)
                    if e == 0:
                        dve.wait_ge(gate_ready, v + 1)
                        wait(dve, x2_ready, v)
                    else:
                        dve.wait_ge(acc_done, i - 1)
                    prev = x1 if e == 0 else acc
                    V.scalar_tensor_tensor(acc[:, b, :], ps_o[e % 2][:, b * D:(b + 1) * D], gate[:, b, e:e + 1],
                                           prev[:, b, :],
                                           ALU.mult, ALU.add).then_inc(acc_done, 1)
                elif name == "ln2_stats":
                    dve.wait_ge(acc_done, RING_STEPS * (v + 1))
                    layernorm_stats(1, acc, v)
                elif name == "ln2_apply":
                    layernorm_apply(1, x2, acc, v, x2_ready)
                elif name == "quantise":
                    dve.wait_ge(xh_ready, v + 1)
                    xh = ps_misc[:, :].rearrange("p (b n) -> p b n", b=UB)
                    V.tensor_reduce(amax[:, :], xh, AX_X, ALU.max, apply_absolute_value=True)\
                        .then_inc(quant_step, 1)
                    dve.wait_ge(quant_step, 4 * v + 1)
                    V.tensor_scalar(xscale[:, :], amax[:, :], 1e-5, 1.0 / QPOS, ALU.max, ALU.mult)\
                        .then_inc(quant_step, 1)
                    dve.wait_ge(quant_step, 4 * v + 2)
                    V.reciprocal(xscale_inv[:, :], xscale[:, :]).then_inc(inv_ready, 1)
                    dve.wait_ge(inv_ready, v + 1)
                    for b in range(UB):
                        last = V.tensor_scalar(rounded[:, b, :], xh[:, b, :], xscale_inv[:, b:b + 1], ROUND,
                                               ALU.mult, ALU.add)
                    last.then_inc(quant_step, 1)
                    dve.wait_ge(quant_step, 4 * v + 3)
                    V.tensor_scalar(clipped[:, :, :], rounded[:, :, :], ROUND - QNEG, ROUND + QPOS, ALU.max,
                                    ALU.min).then_inc(quant_step, 1)
                elif name == "ln3_stats":
                    dve.wait_ge(f_ready, v + 1)
                    for b in range(UB):
                        last = V.scalar_tensor_tensor(f_sb[:, b, :], ps_misc[:, b * D:(b + 1) * D],
                                                      xscale[:, b:b + 1], wscale[:, :], ALU.mult, ALU.mult)
                    last.then_inc(f_scaled, 1)
                    dve.wait_ge(f_scaled, v + 1)
                    V.tensor_tensor(t3[:, :, :], f_sb[:, :, :], x2[:, :, :], ALU.add).then_inc(t3_ready, 1)
                    dve.wait_ge(t3_ready, v + 1)
                    layernorm_stats(2, t3, v)
                elif name == "ln3_apply":
                    dve.wait_ge(s_store, 16 * (v + 1))
                    layernorm_apply(2, out_sb, t3, v, out_ready)

            for b in (taken, e_sb, p_sb):
                last = V.memset(b[:], 0.0)
            last.then_inc(zeroed, 1)
            dve.wait_ge(zeroed, 1)
            walk("dve", step, dve)


_INPUTS = ["x", "xt", "ctx_w", "itok", "wqt", "bq", "wkt", "bk", "wvt", "bv", "wot", "bo", "w1t", "w2t", "ffnt",
           "c_ident", "c_hadamard", "c_causal", "c_heads"]


def kernel(x, ctx_512, itok_BxS2xS_0_7, L0_attn_Wq, L0_attn_bq, L0_attn_Wk, L0_attn_bk, L0_attn_Wv, L0_attn_bv,
           L0_attn_Wo, L0_attn_bo, L0_xattn_proj_in, L0_xattn_proj_out, L0_ffn_weight):
    import numpy as np
    import concourse.bacc as bacc
    from concourse import mybir as mb
    from concourse.bass_utils import run_bass_kernel_spmd

    had = np.array([[1.0]])
    while had.shape[0] < D:
        had = np.block([[had, had], [had, -had]])

    def by_chunk(bias):
        return np.asarray(bias).reshape(CD, P).T

    row, col = np.arange(P)[:, None], np.arange(P)[None, :]
    arrays = {
        "x": x, "xt": np.asarray(x).reshape(BATCH * SEQ, D).T, "ctx_w": np.asarray(ctx_512).transpose(0, 2, 1),
        "itok": np.asarray(itok_BxS2xS_0_7).transpose(0, 2, 1),
        "wqt": np.asarray(L0_attn_Wq).T, "bq": by_chunk(L0_attn_bq),
        "wkt": np.asarray(L0_attn_Wk).T, "bk": by_chunk(L0_attn_bk),
        "wvt": np.asarray(L0_attn_Wv).T, "bv": by_chunk(L0_attn_bv), "wot": np.asarray(L0_attn_Wo).T, "bo": L0_attn_bo,
        "w1t": np.asarray(L0_xattn_proj_in).transpose(0, 2, 1),
        "w2t": np.asarray(L0_xattn_proj_out).transpose(0, 2, 1),
        "ffnt": np.asarray(L0_ffn_weight).T,
        "c_ident": np.eye(P, dtype=np.float32),
        "c_hadamard": (had / np.sqrt(D)).astype(np.float32),
        "c_causal": np.tile(np.where(col[:, :QB] > row % QB, MASKED, 0.0), (1, HALF)).astype(np.float32),
        "c_heads": (row // DH == col[:, :HG]).astype(np.float32),
    }
    arrays = {f"in_{n}": np.ascontiguousarray(arrays[n]) for n in _INPUTS}
    nc = bacc.Bacc("TRN2", target_bir_lowering=False, num_devices=1)
    args = [nc.dram_tensor(n, a.shape, mb.dt.from_np(a.dtype), kind="ExternalInput").ap() for n, a in arrays.items()]
    out = nc.dram_tensor("out", (BATCH, SEQ, D), mb.dt.float32, kind="ExternalOutput").ap()
    decoder_layer(nc, *args, out)
    r = run_bass_kernel_spmd(nc, [arrays], core_ids=[0])
    return r.results[0]["out"]
```
